# Optimizing a Trainium2 kernel written in Bass

```python
import numpy as np
import jax
import jax.numpy as jnp

def _softmax(x, axis=-1):
    return jax.nn.softmax(x, axis=axis)

def _gelu(x):
    return jax.nn.gelu(x, approximate=True)

def _silu(x):
    return jax.nn.silu(x)

def _sigmoid(x):
    return jax.nn.sigmoid(x)

def _layernorm(x, axis=-1, eps=1e-05):
    m = jnp.mean(x, axis=axis, keepdims=True)
    v = jnp.var(x, axis=axis, keepdims=True)
    return (x - m) / jnp.sqrt(v + eps)

def _scatter_add(tgt, idx, src, axis=0):
    return tgt.at[idx].add(src)

def _segment_sum(src, seg, n):
    return jax.ops.segment_sum(src, seg, n)
kernel_name = 'mk_gps_d1_gnn_r8_eb5b8d'

def setup_inputs(seed: int=0):
    np.random.seed(seed)
    _w = jnp.asarray

    def _rec_inputs():
        import jax
        import jax.numpy as jnp
        _gk = jax.random.key(seed)
        x = -0.0003713 + 1 * jax.random.normal(jax.random.fold_in(_gk, 1), (6250, 256), jnp.float32)
        _s = jax.random.randint(jax.random.fold_in(_gk, 2), (50000,), 0, 6250, jnp.int32)
        _d = jax.random.randint(jax.random.fold_in(_gk, 3), (50000,), 0, 6250, jnp.int32)
        _loop = jnp.arange(6250, dtype=jnp.int32)
        src = jnp.concatenate([_s, _d, _loop])
        dst = jnp.concatenate([_d, _s, _loop])
        _o = jnp.argsort(dst, stable=True)
        src = src[_o]
        dst = dst[_o]
        return (x, src, dst)
    x, src, dst = _rec_inputs()

    def _L0_gnn_setup():
        import jax, jax.numpy as jnp
        import numpy as np
        N, IN_CH, HEADS, OUT_CH, E = (6250, 256, 4, 64, 100000)
        key = jax.random.key(seed)
        k1, k2, k3, k4, k5 = jax.random.split(key, 5)
        x = jax.random.normal(k1, (N, IN_CH), dtype=jnp.float32)
        edge_index = jax.random.randint(k2, (2, E), 0, N, dtype=jnp.int64)
        bw = float(np.sqrt(6.0 / (IN_CH + HEADS * OUT_CH)))
        ba = float(np.sqrt(6.0 / (HEADS + OUT_CH)))
        weight = jax.random.uniform(k3, (IN_CH, HEADS * OUT_CH), jnp.float32, -bw, bw)
        attn_l = jax.random.uniform(k4, (HEADS, OUT_CH), jnp.float32, -ba, ba)
        attn_r = jax.random.uniform(k5, (HEADS, OUT_CH), jnp.float32, -ba, ba)
        return {'x': x, 'edge_index': edge_index, 'weight': weight, 'attn_l': attn_l, 'attn_r': attn_r}
    _L0_gnn_all = _L0_gnn_setup()
    _L0_gnn_in = {k: v for k, v in _L0_gnn_all.items() if k in ('weight', 'attn_l', 'attn_r')}
    del _L0_gnn_all

    def _L0_mix_setup():
        import jax, jax.numpy as jnp
        import numpy as np
        B, N, C, H = (8, 2048, 256, 8)
        D = C // H
        GH = C // 4
        key = jax.random.key(seed)
        ks = jax.random.split(key, 6)
        s = 0.02
        return {'x': jax.random.normal(ks[0], (B, N, C), dtype=jnp.float32), 'Wqkv': jax.random.normal(ks[1], (C, 3 * C), dtype=jnp.float32) * s, 'Wproj': jax.random.normal(ks[2], (C, C), dtype=jnp.float32) * s, 'bproj': jnp.zeros((C,), dtype=jnp.float32), 'ln_g': jnp.ones((C,), dtype=jnp.float32), 'ln_b': jnp.zeros((C,), dtype=jnp.float32), 'Wg1': jax.random.normal(ks[3], (C, GH), dtype=jnp.float32) * s, 'bg1': jnp.zeros((GH,), dtype=jnp.float32), 'Wg2': jax.random.normal(ks[4], (GH, C), dtype=jnp.float32) * s, 'bg2': jnp.zeros((C,), dtype=jnp.float32)}
    _L0_mix_all = _L0_mix_setup()
    _L0_mix_in = {k: v for k, v in _L0_mix_all.items() if k in ('Wqkv', 'Wproj', 'bproj', 'ln_g', 'ln_b', 'Wg1', 'bg1', 'Wg2', 'bg2')}
    del _L0_mix_all

    def _L0_ffn_setup():
        import jax, jax.numpy as jnp
        import numpy as np
        TOP_K = 2
        LN_EPS = 1e-05
        key = jax.random.key(seed)
        ks = jax.random.split(key, 8)
        B, S, D, E, H = (16, 1024, 256, 8, 1024)
        x = jax.random.normal(ks[0], (B, S, D), dtype=jnp.float32)
        Wr = jax.random.normal(ks[1], (D, E), dtype=jnp.float32) * 0.1
        br = jnp.zeros((E,), dtype=jnp.float32)
        ln_g = jnp.ones((E, D), dtype=jnp.float32)
        ln_b = jnp.zeros((E, D), dtype=jnp.float32)
        W1 = jax.random.normal(ks[2], (E, D, H), dtype=jnp.float32) * (1.0 / np.sqrt(D))
        b1 = jnp.zeros((E, H), dtype=jnp.float32)
        W2 = jax.random.normal(ks[3], (E, H, D), dtype=jnp.float32) * (1.0 / np.sqrt(H))
        b2 = jnp.zeros((E, D), dtype=jnp.float32)
        return {'x': x, 'Wr': Wr, 'br': br, 'ln_g': ln_g, 'ln_b': ln_b, 'W1': W1, 'b1': b1, 'W2': W2, 'b2': b2}
    _L0_ffn_all = _L0_ffn_setup()
    _L0_ffn_in = {k: v for k, v in _L0_ffn_all.items() if k in ('Wr', 'br', 'ln_g', 'ln_b', 'W1', 'b1', 'W2', 'b2')}
    del _L0_ffn_all
    return {'x': x, 'src': src, 'dst': dst, 'L0_gnn_weight': _L0_gnn_in['weight'], 'L0_gnn_attn_l': _L0_gnn_in['attn_l'], 'L0_gnn_attn_r': _L0_gnn_in['attn_r'], 'L0_mix_Wqkv': _L0_mix_in['Wqkv'], 'L0_mix_Wproj': _L0_mix_in['Wproj'], 'L0_mix_bproj': _L0_mix_in['bproj'], 'L0_mix_ln_g': _L0_mix_in['ln_g'], 'L0_mix_ln_b': _L0_mix_in['ln_b'], 'L0_mix_Wg1': _L0_mix_in['Wg1'], 'L0_mix_bg1': _L0_mix_in['bg1'], 'L0_mix_Wg2': _L0_mix_in['Wg2'], 'L0_mix_bg2': _L0_mix_in['bg2'], 'L0_ffn_Wr': _L0_ffn_in['Wr'], 'L0_ffn_br': _L0_ffn_in['br'], 'L0_ffn_ln_g': _L0_ffn_in['ln_g'], 'L0_ffn_ln_b': _L0_ffn_in['ln_b'], 'L0_ffn_W1': _L0_ffn_in['W1'], 'L0_ffn_b1': _L0_ffn_in['b1'], 'L0_ffn_W2': _L0_ffn_in['W2'], 'L0_ffn_b2': _L0_ffn_in['b2']}

def reference(x, src, dst, L0_gnn_weight, L0_gnn_attn_l, L0_gnn_attn_r, L0_mix_Wqkv, L0_mix_Wproj, L0_mix_bproj, L0_mix_ln_g, L0_mix_ln_b, L0_mix_Wg1, L0_mix_bg1, L0_mix_Wg2, L0_mix_bg2, L0_ffn_Wr, L0_ffn_br, L0_ffn_ln_g, L0_ffn_ln_b, L0_ffn_W1, L0_ffn_b1, L0_ffn_W2, L0_ffn_b2):
    import jax
    import jax.numpy as jnp

    def _L0_gnn_ref(x, edge_index, weight, attn_l, attn_r):
        import jax, jax.numpy as jnp
        import numpy as np
        N, IN_CH, HEADS, OUT_CH, E = (6250, 256, 4, 64, 100000)
        heads, out_ch = attn_l.shape
        n = x.shape[0]
        xt = jnp.matmul(x, weight).reshape(-1, heads, out_ch)
        row, col = (edge_index[0], edge_index[1])
        alpha_l = jnp.einsum('ehd,hd->eh', xt[row], attn_l)
        alpha_r = jnp.einsum('ehd,hd->eh', xt[col], attn_r)
        alpha = jax.nn.softmax(jax.nn.leaky_relu(alpha_l + alpha_r, 0.01), axis=1)
        tmp = jnp.einsum('nh,nhd->nd', alpha[:n], xt[col[:n]])
        out = jnp.broadcast_to(tmp[:, None, :], (n, heads, out_ch))
        return out.reshape(n, heads * out_ch)

    def _L0_mix_ref(x, Wqkv, Wproj, bproj, ln_g, ln_b, Wg1, bg1, Wg2, bg2):
        import jax, jax.numpy as jnp
        import numpy as np
        B, N, C, H = (8, 2048, 256, 8)
        D = C // H
        GH = C // 4
        b, n, c = x.shape
        h, d = (H, D)
        qkv = (x @ Wqkv).reshape(b, n, 3, h, d)
        q, k, v = (qkv[:, :, 0], qkv[:, :, 1], qkv[:, :, 2])
        k = jax.nn.softmax(k, axis=1)
        context = jnp.einsum('bnhd,bnhv->bhdv', k, v)
        out = jnp.einsum('bnhd,bhdv->bnhv', q, context).reshape(b, n, c)
        mu = jnp.mean(x, axis=-1, keepdims=True)
        var = jnp.var(x, axis=-1, keepdims=True)
        xn = (x - mu) * jax.lax.rsqrt(var + 1e-05) * ln_g + ln_b
        hgate = jax.nn.gelu(xn @ Wg1 + bg1, approximate=False)
        gate = jax.nn.sigmoid(hgate @ Wg2 + bg2)
        return out * gate @ Wproj + bproj

    def _L0_ffn_ref(x, Wr, br, ln_g, ln_b, W1, b1, W2, b2):
        import jax, jax.numpy as jnp
        import numpy as np
        TOP_K = 2
        LN_EPS = 1e-05
        B, S, D = x.shape
        N = B * S
        xt = x.reshape(N, D)
        logits = xt @ Wr + br
        probs = jax.nn.softmax(logits, axis=-1)
        top_p, top_idx = jax.lax.top_k(probs, TOP_K)
        weights = top_p / top_p.sum(axis=-1, keepdims=True)
        mu = xt.mean(axis=-1, keepdims=True)
        var = ((xt - mu) ** 2).mean(axis=-1, keepdims=True)
        xn = (xt - mu) * jax.lax.rsqrt(var + LN_EPS)
        xe = xn[None, :, :] * ln_g[:, None, :] + ln_b[:, None, :]
        h = jax.nn.gelu(jnp.einsum('end,edh->enh', xe, W1) + b1[:, None, :], approximate=False)
        y = jnp.einsum('enh,ehd->end', h, W2) + b2[:, None, :]
        y_tok = jnp.transpose(y, (1, 0, 2))
        sel = jnp.take_along_axis(y_tok, top_idx[:, :, None], axis=1)
        out = (weights[:, :, None] * sel).sum(axis=1)
        return out.reshape(B, S, D)
    edge_index = jnp.stack([src, dst])
    xn = _layernorm(x, axis=-1)
    x = x + _L0_gnn_ref(xn, edge_index, L0_gnn_weight, L0_gnn_attn_l, L0_gnn_attn_r) + _L0_mix_ref(xn[None], L0_mix_Wqkv, L0_mix_Wproj, L0_mix_bproj, L0_mix_ln_g, L0_mix_ln_b, L0_mix_Wg1, L0_mix_bg1, L0_mix_Wg2, L0_mix_bg2)[0]
    x = x + _L0_ffn_ref(_layernorm(x, axis=-1)[None], L0_ffn_Wr, L0_ffn_br, L0_ffn_ln_g, L0_ffn_ln_b, L0_ffn_W1, L0_ffn_b1, L0_ffn_W2, L0_ffn_b2)[0]
    return x

_drawn_inputs = setup_inputs


def setup_inputs(seed=0):
    import zlib

    import numpy as np

    out = dict(_drawn_inputs(seed))
    spreads = {'L0_mix_bproj': (0.0, 0.1),
     'L0_mix_ln_g': (1.0, 0.6),
     'L0_mix_ln_b': (0.0, 0.8),
     'L0_mix_bg1': (0.0, 0.8),
     'L0_mix_bg2': (0.0, 0.8),
     'L0_ffn_br': (0.0, 0.1),
     'L0_ffn_ln_g': (1.0, 0.2),
     'L0_ffn_ln_b': (0.0, 0.456),
     'L0_ffn_b1': (0.0, 0.452),
     'L0_ffn_b2': (0.0, 0.317)}
    factors = {'L0_mix_Wqkv': 5.568, 'L0_mix_Wproj': 6.181, 'L0_mix_Wg1': 8.0, 'L0_mix_Wg2': 8.0}
    for name, (base, spread) in spreads.items():
        noise = np.random.default_rng([zlib.crc32(name.encode()), seed]).standard_normal(out[name].shape)
        drawn = base * np.exp(spread * noise) if base else spread * noise
        out[name] = jnp.asarray(drawn.astype(out[name].dtype))
    for name, factor in factors.items():
        out[name] = (out[name] * factor).astype(out[name].dtype)
    return out
```

```python
import concourse.bass as bass
from concourse import mybir
from contextlib import ExitStack
from collections import namedtuple

P = 128
N, C = 6250, 256
NT = 50
NP = NT * P
LAST = N // P
NK = C // P
HG, DG = 4, 64
DM = 32
GH = C // 4
NE, HID = 8, 1024
HJ = HID // 2
HC = HJ // P
FT = (2 * N + NE * (P - 1)) // P
ROW = C + 2 * HG
WM = C + ROW + GH
EPS = 1e-5
BIG = 3.0e38

Tile = namedtuple("Tile", "t u i")


def back(tile, lag):
    t, u = tile.t - lag, (tile.u - lag) % 2
    if isinstance(t, int) and not 0 <= t < NT:
        return None
    return Tile(t, u, tile.i + (tile.u - lag - u) // 2)


def sweep(eng, last_lag, step):
    lead = 2 * ((last_lag + 1) // 2)
    for s in range(lead):
        step(Tile(s, s % 2, s // 2))
    with eng.Fori(lead // 2, NT // 2) as i:
        for u in range(2):
            step(Tile(2 * i + u, u, i))
    for s in range(NT, NT + last_lag):
        step(Tile(s, s % 2, s // 2))


def done(tile):
    return tile.t + 3


def freed(tile):
    return tile.t + 1


def landed(tile, each=16):
    return tile.i * each + 2 * each


def left(tile, each=16):
    return tile.i * each + each


def gps_layer(nc, x, src, dst, wk, wqT, wv, wgnn, attn, wproj, bproj, vecs, wg1, bg1, wg2,
              wr, br, flng, flnb, w1, b1, w2, b2, out, xt_table, al_table, x4_table):
    fp32, i32 = mybir.dt.float32, mybir.dt.int32
    ALU = mybir.AluOpType
    ACT = mybir.ActivationFunctionType
    AX = mybir.AxisListType
    ds = bass.ds

    with ExitStack() as ctx:
        def sb(name, shape, dt=fp32):
            return ctx.enter_context(nc.sbuf_tensor(name, shape, dt))

        R1 = sb("R1", [P, 2 * NK * NP])
        kT_all, v_all = R1[:, 0:NK * NP], R1[:, NK * NP:2 * NK * NP]
        w1_all = R1[:, 0:NE * NK * HID]
        b1_all = R1[:, NE * NK * HID:NE * (NK + 1) * HID]
        R2 = sb("R2", [P, NE * NK * HID])
        xnT_all, hg_all = R2[:, 0:NK * NP], R2[:, NK * NP:NK * NP + NT * GH]
        w2_all = R2
        RA = sb("RA", [P, NK * WM + NK * C + 2 * C])
        wm = RA[:, 0:NK * WM].rearrange("p (k c) -> p k c", k=NK)
        wk_sb = RA[:, NK * WM:NK * (WM + C)].rearrange("p (k c) -> p k c", k=NK)
        attn_sb = RA[:, NK * (WM + C):NK * (WM + C) + 2 * C].rearrange("p (s c) -> p s c", s=2)
        b2_all = RA[:, 0:NE * C]
        R3 = sb("R3", [P, 5120])

        def pair(at, width):
            return R3[:, at:at + 2 * width].rearrange("p (u c) -> p u c", u=2)

        x_sb, xn, xnT, xt_sb = pair(0, C), pair(512, C), pair(1024, C), pair(1536, ROW)
        sg, og, x2, x4 = pair(2064, C), pair(2576, C), pair(3088, C), pair(3600, C)
        tmp, hgT, hgb, hgpre = pair(4112, DG), pair(4240, P), pair(4496, GH), pair(4624, GH)
        ek, ekT = sg, og
        rv, ohb, ttb = pair(0, 2 * FT), pair(512, P), R3[:, 1024:1024 + NE * P]
        xs, xsT = R3[:, 0:C], R3[:, C:2 * C]
        hpre, hid, hidT = R3[:, 512:512 + HID], R3[:, 1536:1536 + HID], R3[:, 2560:2560 + HID]
        y1, yw = R3[:, 3584:3584 + C], R3[:, 3840:3840 + C]
        lnb_b = R3[:, 4096:4096 + NK * P]
        wqT_sb, wproj_sb, m1 = (sb(n, [P, NK, C]) for n in ("wqT_sb", "wproj_sb", "m1"))
        wg2_sb = sb("wg2_sb", [GH, C])
        bproj_sb, bg1_sb, br_sb = sb("bproj_sb", [P, C]), sb("bg1_sb", [P, GH]), sb("br_sb", [P, NE])
        vec = sb("vec", [P, 3, NK])
        wr_sb = sb("wr_sb", [P, NK, NE])
        flng_sb, flnb_sb = sb("flng_sb", [P, NK * NE]), sb("flnb_sb", [P, NK * NE])
        ident, ones, upper = sb("ident", [P, P]), sb("ones", [P, P]), sb("upper", [P, P])
        cols = sb("cols", [P, P])
        ctx_bd = sb("ctx_bd", [P, NK, P])
        src_i, dst_i = sb("src_i", [P, NT], i32), sb("dst_i", [P, NT], i32)
        idx = sb("idx", [P, 4], i32)
        st, mv = sb("st", [P, 2, 6]), sb("mv", [P, 2, 2])
        va, vb, rs, r2 = (sb(n, [P, 2, w]) for n, w in (("va", 3), ("vb", 3), ("rs", 3), ("r2", 1)))
        cmul, cadd, cexp = sb("cmul", [P, 3]), sb("cadd", [P, 3]), sb("cexp", [P, 3])
        kmax, nkmax = sb("kmax", [P, NK, NT]), sb("nkmax", [P, NK])
        ksum, kinv = sb("ksum", [P, NK * NT]), sb("kinv", [P, 2, NK])
        g2, lg, sm = sb("g2", [P, 2, HG]), sb("lg", [P, 2, 3 * HG]), sb("sm", [P, 2, 4])
        TE = NT * NE
        logits = wqT_sb[:, :, :].rearrange("p k c -> p (k c)")[:, 0:TE]
        work, chosen, oh0, oh1 = (R3[:, 2048 + j * TE:2048 + (j + 1) * TE] for j in range(4))
        oh = [oh0, oh1]
        pos = R3[:, 2048 + 4 * TE:2048 + 5 * TE + NE]
        at = NE * (NK + 1) * HID
        tok = R1[:, at:at + 16 * NT].rearrange("p (j t) -> p j t", t=NT)
        tok_i = R3[:, 4352:4352 + 6 * NT].bitcast(i32).rearrange("p (j t) -> p j t", t=NT)
        gidx, sidx, slot_w, te = (R3[:, 4652 + j * FT:4652 + (j + 1) * FT] for j in range(4))
        gidx, sidx, te = gidx.bitcast(i32), sidx.bitcast(i32), te[0:1, :].bitcast(i32)
        sl = R3[:, 768:768 + 2 * FT].rearrange("p (j t) -> p j t", j=2)
        desc = sb("desc", [P, NE])
        small = sb("small", [P, 4, NE])
        small_i = sb("small_i", [P, 2, NE], i32)
        dummy = sb("dummy_row", [P, 1])
        zrow = sb("zrow", [P, C])
        bank = [ctx.enter_context(nc.psum_tensor(f"bank{b}", [P, 512], fp32)) for b in range(8)]

        at_start = {}

        def counts(prefix, names, start):
            made = [ctx.enter_context(nc.semaphore(f"{prefix}_{n}")) for n in names.split()]
            for s in made:
                at_start[id(s)] = (s, start)
            return made

        a_stats, a_mv, a_v1, a_v2, a_pow, a_r2, a_xn, a_tr, a_xnT, a_all = counts(
            "a", "stats mv v1 v2 pow r2 xn tr xnT all", 2)
        a_kmm, a_vmm, a_gmm, a_kc, a_vc, a_row, a_hg, a_gelu = counts(
            "a", "kmm vmm gmm kc vc row hg gelu", 2)
        k_exp, k_tr, k_cp, k_mm = counts("k", "exp tr cp mm", 2)
        b_omm, b_htr, b_hgT, b_gmm, b_sg, b_og, b_pmm = counts("b", "omm htr hgT gmm sg og pmm", 2)
        b_hgb, b_idx, b_xb, b_al, b_lk, b_alpha, b_exp = counts("b", "hgb idx xb al lk alpha exp", 2)
        b_g0, b_g1, b_g2, b_gn, b_mix, b_x2, b_stats, b_mv = counts("b", "g0 g1 g2 gn mix x2 stats mv", 2)
        b_v1, b_v2, b_rstd, b_x3, b_x4, b_tr, b_xnT, b_lmm, b_lc = counts(
            "b", "v1 v2 rstd x3 x4 tr xnT lmm lc", 2)
        t_oh, t_idx, t_w, t_mm = counts("t", "oh idx w mm", 2)
        w_le, w_mm0, w_mm1, w_c0, w_c1, w_s = counts("w", "le mm0 mm1 c0 c1 s", 1)
        w_mm, w_c = (w_mm0, w_mm1), (w_c0, w_c1)
        f_gi, f_si, f_x, f_xc, f_y1, f_yw = counts("f", "gi si x xc y1 yw", 1)
        f_h, f_hb, f_ge, f_t, f_tc, f_y = (counts("f", f"{n}0 {n}1", 1) for n in ("hmm", "hb", "ge", "tr", "tc", "ymm"))
        a_in, b_in = counts("a", "in0 in1", 16), counts("b", "in0 in1", 16)
        a_tab, b_out = counts("a", "tab0 tab1", 32), counts("b", "out0 out1", 32)
        b_gat, (f_gat, f_add) = counts("b", "gat0 gat1", 0), counts("f", "gat add", 0)
        (s_w, s_pool, s_lnb, s_bg, s_bgc, s_prep, s_kmax, s_csum, s_ctx, s_m1, s_m1c, s_w1, s_w2, s_b1, s_b2,
         s_r, s_chosen, s_tot, s_ttb, s_pos, s_diff, s_exp, s_table, s_slots, s_dummy) = counts(
            "s", "w pool lnb bg bgc prep kmax csum ctx m1 m1c w1 w2 b1 b2 r chosen tot ttb pos diff exp table slots dummy", 0)

        s_held = counts("s", "held_dve held_pe held_pool", 0)

        block = ctx.enter_context(nc.Block())
        x_t, out_t, xt_t, al_t, x4_t = (a.rearrange("(t p) c -> t p c", p=P)
                                        for a in (x, out, xt_table, al_table, x4_table))

        def tile_of(all_tokens, k, tile):
            return all_tokens[:, ds(tile.t * P + k * NP, P)]

        @block.sync
        def _(sp):
            for t, a in ((wm[:, :, 0:C], wv), (wm[:, :, C:2 * C], wgnn), (wm[:, :, C + ROW:WM], wg1),
                         (wk_sb, wk), (attn_sb, attn), (wqT_sb, wqT), (wproj_sb, wproj), (wg2_sb, wg2),
                         (bproj_sb, bproj), (bg1_sb, bg1), (br_sb, br), (vec, vecs), (wr_sb, wr),
                         (flng_sb, flng), (flnb_sb, flnb), (src_i, src), (dst_i, dst)):
                sp.dma_start(t if isinstance(t, bass.AP) else t[:], a).then_inc(s_w, 16)

            def load_a(s):
                sp.lower_val(s.t), sp.lower_val(freed(s)), sp.lower_val(landed(s))
                sp.wait_ge(a_xn, freed(s))
                sp.dma_start(x_sb[:, s.u, :], x_t[s.t, :, :]).then_inc(a_in[s.u], 16)

            sweep(sp, 0, load_a)
            sp.wait_ge(s_ctx, 1)
            sp.dma_start(w1_all, w1).then_inc(s_w1, 16)
            sp.dma_start(b1_all[0:1, :], b1).then_inc(s_b1, 16)
            sp.dma_start(b2_all, b2).then_inc(s_b2, 16)

            def rows_b(s):
                sp.lower_val(s.t), sp.lower_val(freed(s)), sp.lower_val(s.i)
                if e := back(s, 0):
                    sp.wait_ge(b_x2, freed(e))
                    sp.dma_start(x_sb[:, e.u, :], x_t[e.t, :, :]).then_inc(b_in[e.u], 16)
                if e := back(s, 2):
                    sp.lower_val(done(e)), sp.lower_val(e.t)
                    sp.wait_ge(b_x2, done(e))
                    sp.dma_start(out_t[e.t, :, :], x2[:, e.u, :]).then_inc(b_out[e.u], 16)
                    sp.wait_ge(b_x4, done(e))
                    sp.dma_start(x4_t[e.t, :, :], x4[:, e.u, :]).then_inc(b_out[e.u], 16)

            sp.wait_ge(a_xn, NT + 2)
            sweep(sp, 2, rows_b)
            sp.wait_ge(b_omm, NT + 2)
            sp.wait_ge(b_hgb, NT + 2)
            sp.dma_start(w2_all[:, :], w2).then_inc(s_w2, 16)
            sp.dma_start(out[NP:NP + P, :], zrow[:, :]).then_inc(s_dummy, 16)
            sp.wait_ge(s_dummy, 16)
            sp.wait_ge(f_add, 16 * FT)
            for u in range(2):
                sp.wait_ge(b_out[u], 32 * (NT // 2 + 1))

        @block.gpsimd
        def _(pool):
            for s, start in at_start.values():
                if start:
                    pool.sem_inc(s, start)
            nc.gpsimd.memset(ones[:, :], 1.0).then_inc(s_pool, 1)
            nc.gpsimd.memset(ident[:, :], 0.0).then_inc(s_pool, 1)
            nc.gpsimd.iota(cols[:, :], pattern=[[1, P]], base=0, channel_multiplier=0,
                           allow_small_or_imprecise_dtypes=True).then_inc(s_pool, 1)
            nc.gpsimd.iota(desc[:, :], pattern=[[-1, NE]], base=NE, channel_multiplier=0,
                           allow_small_or_imprecise_dtypes=True).then_inc(s_pool, 1)
            nc.gpsimd.iota(dummy[:, :], pattern=[[0, 1]], base=NP + 1, channel_multiplier=1,
                           allow_small_or_imprecise_dtypes=True).then_inc(s_pool, 1)
            nc.gpsimd.memset(ctx_bd[:, :, :], 0.0).then_inc(s_pool, 1)
            nc.gpsimd.memset(zrow[:, :], 0.0).then_inc(s_pool, 1)
            for j, (m, a, e) in enumerate(((1.0, EPS, -0.5), (1.0 + EPS, EPS * EPS, -0.5), (1.0, EPS, 0.5))):
                nc.gpsimd.memset(cmul[:, j:j + 1], m).then_inc(s_pool, 1)
                nc.gpsimd.memset(cadd[:, j:j + 1], a).then_inc(s_pool, 1)
                nc.gpsimd.memset(cexp[:, j:j + 1], e).then_inc(s_pool, 1)
            pool.wait_ge(s_pool, 16)
            nc.gpsimd.affine_select(out=ident[:, :], in_=ident[:, :], compare_op=ALU.not_equal, fill=1.0, base=0,
                                    pattern=[[-1, P]], channel_multiplier=1).then_inc(s_pool, 1)
            nc.gpsimd.affine_select(out=upper[:, :], in_=ones[:, :], compare_op=ALU.is_gt, fill=0.0, base=0,
                                    pattern=[[1, P]], channel_multiplier=-1).then_inc(s_pool, 1)

            def powers(s, mv_sem, s1, s2, s3, freed_by):
                u = s.u
                var = mv[:, u, 1:2].to_broadcast([P, 3])
                pool.wait_ge(mv_sem, done(s))
                nc.gpsimd.tensor_tensor(va[:, u, :], var, cmul[:, :], ALU.mult).then_inc(s1, 1)
                pool.wait_ge(s1, done(s))
                nc.gpsimd.tensor_tensor(vb[:, u, :], va[:, u, :], cadd[:, :], ALU.add).then_inc(s2, 1)
                pool.wait_ge(s2, done(s))
                pool.wait_ge(freed_by, freed(s))
                nc.gpsimd.tensor_tensor(rs[:, u, :], vb[:, u, :], cexp[:, :], ALU.pow).then_inc(s3, 1)

            def step_a(s):
                if back(s, 0):
                    powers(s, a_mv, a_v1, a_v2, a_pow, a_xn)
                    pool.wait_ge(a_pow, done(s))
                    pool.wait_ge(a_hg, freed(s))
                    nc.gpsimd.tensor_tensor(r2[:, s.u, :], rs[:, s.u, 1:2], rs[:, s.u, 2:3], ALU.mult).then_inc(a_r2, 1)
                if e := back(s, 2):
                    pool.wait_ge(a_xnT, done(e))
                    nc.gpsimd.tensor_copy(xnT_all.rearrange("p (k n) -> p k n", k=NK)[:, :, ds(e.t * P, P)],
                                          xnT[:, e.u, :].rearrange("p (k n) -> p k n", k=NK)).then_inc(a_all, 1)

            sweep(pool, 2, step_a)
            pool.wait_ge(s_ctx, 1)
            nc.gpsimd.iota(tok[:, 0, :], pattern=[[P, NT]], base=0, channel_multiplier=1,
                           allow_small_or_imprecise_dtypes=True).then_inc(s_pool, 1)
            pool.wait_ge(s_w, 17 * 16)
            for u in range(2):
                pool.wait_ge(a_tab[u], 32 * (NT // 2 + 1))

            def step_b(s):
                if back(s, 0):
                    u = s.u
                    pool.wait_ge(b_gn, freed(s))
                    nc.gpsimd.tensor_copy(idx[:, 2 * u:2 * u + 1], dst_i[:, ds(s.t, 1)])
                    nc.gpsimd.tensor_copy(idx[:, 2 * u + 1:2 * u + 2], src_i[:, ds(s.t, 1)]).then_inc(b_idx, 1)
                    pool.wait_ge(b_idx, done(s))
                    pool.sem_inc(s_held[2], 1)
                    nc.gpsimd.indirect_dma_start(out=xt_sb[:, u, :], out_offset=None, in_=xt_table,
                                                 in_offset=bass.IndirectOffsetOnAxis(ap=idx[:, 2 * u:2 * u + 1], axis=0)
                                                 ).then_inc(b_gat[u], 16)
                    nc.gpsimd.indirect_dma_start(out=g2[:, u, :], out_offset=None, in_=al_table,
                                                 in_offset=bass.IndirectOffsetOnAxis(ap=idx[:, 2 * u + 1:2 * u + 2], axis=0)
                                                 ).then_inc(b_gat[u], 16)
                    pool.wait_ge(b_htr, freed(s))
                    nc.gpsimd.tensor_copy(hgb[:, u, :], hg_all[:, ds(s.t * GH, GH)]).then_inc(b_hgb, 1)
                if e := back(s, 1):
                    pool.wait_ge(b_in[e.u], landed(e))
                    nc.gpsimd.tensor_tensor(x_sb[:, e.u, :], x_sb[:, e.u, :], bproj_sb[:, :], ALU.add).then_inc(b_xb, 1)
                if e := back(s, 2):
                    powers(e, b_mv, b_v1, b_v2, b_rstd, b_x4)

            pool.wait_ge(a_gelu, NT + 2)
            sweep(pool, 2, step_b)

            pool.wait_ge(s_slots, 1)
            for u in range(2):
                pool.wait_ge(b_out[u], 32 * (NT // 2 + 1))
            pool.wait_ge(s_dummy, 16)

            def gather(t):
                pool.wait_ge(f_x, t + 1)
                nc.gpsimd.tensor_copy(idx[:, 0:1], gidx[:, ds(t, 1)]).then_inc(f_gi, 1)
                pool.wait_ge(f_gi, t + 2)
                pool.sem_inc(s_held[2], 1)
                nc.gpsimd.indirect_dma_start(out=xs, out_offset=None, in_=x4_table,
                                             in_offset=bass.IndirectOffsetOnAxis(ap=idx[:, 0:1], axis=0)
                                             ).then_inc(f_gat, 16)

            def add(t):
                if not (isinstance(t, int) and t == 0):
                    pool.wait_ge(f_add, 16 * t)
                nc.gpsimd.tensor_copy(idx[:, 1:2], sidx[:, ds(t, 1)]).then_inc(f_si, 1)
                pool.wait_ge(f_si, t + 2)
                pool.wait_ge(f_yw, t + 2)
                pool.sem_inc(s_held[2], 1)
                nc.gpsimd.indirect_dma_start(out=out, out_offset=bass.IndirectOffsetOnAxis(ap=idx[:, 1:2], axis=0),
                                             in_=yw, in_offset=None, compute_op=ALU.add).then_inc(f_add, 16)

            for t in range(3):
                gather(t)
            add(0)
            with pool.Fori(3, FT) as t:
                gather(t)
                add(t - 2)
            add(FT - 2)
            add(FT - 1)

        @block.scalar
        def _(act):
            def step_a(s):
                if back(s, 0):
                    act.wait_ge(a_tr, done(s))
                    act.wait_ge(a_gmm, freed(s))
                    act.wait_ge(a_all, freed(s))
                    nc.scalar.copy(xnT[:, s.u, :], bank[s.u][:, 0:C]).then_inc(a_xnT, 1)
                if e := back(s, 1):
                    u = e.u
                    act.wait_ge(a_kmm, done(e))
                    nc.scalar.copy(kT_all.rearrange("p (k n) -> p k n", k=NK)[:, :, ds(e.t * P, P)],
                                   bank[2 + u][:, 0:C].rearrange("p (k n) -> p k n", k=NK)).then_inc(a_kc, 1)
                    act.wait_ge(a_vmm, done(e))
                    nc.scalar.copy(v_all[:, ds(e.t * C, C)], bank[4 + u][:, 0:C]).then_inc(a_vc, 1)
                    act.wait_ge(a_row, done(e))
                    act.dma_start(xt_t[e.t, :, :], xt_sb[:, u, :]).then_inc(a_tab[u], 16)
                    act.dma_start(al_t[e.t, :, :], xt_sb[:, u, C:C + HG]).then_inc(a_tab[u], 16)
                    act.wait_ge(a_hg, done(e))
                    nc.scalar.activation(hg_all[:, ds(e.t * GH, GH)], hgpre[:, u, :], ACT.Gelu).then_inc(a_gelu, 1)

            sweep(act, 1, step_a)
            act.wait_ge(s_kmax, 3)

            def step_k(s):
                act.wait_ge(k_tr, freed(s))
                for f in range(NK):
                    last = nc.scalar.activation(ek[:, s.u, f * P:(f + 1) * P], tile_of(kT_all, f, s), ACT.Exp,
                                                bias=nkmax[:, f:f + 1], accum_out=ksum[:, ds(s.t + f * NT, 1)])
                last.then_inc(k_exp, 1)

            sweep(act, 0, step_k)
            act.wait_ge(s_m1, 1)
            nc.scalar.copy(m1[:, :, :].rearrange("p k c -> p (k c)"), bank[4][:, 0:NK * C]).then_inc(s_m1c, 1)

            def step_b(s):
                here = back(s, 0)
                e = back(s, 2)
                if here:
                    act.wait_ge(b_htr, done(s))
                    act.wait_ge(b_gmm, freed(s))
                    nc.scalar.copy(hgT[0:GH, s.u, :], bank[2 + s.u][0:GH, 0:P]).then_inc(b_hgT, 1)
                if e:
                    act.wait_ge(b_tr, done(e))
                    act.wait_ge(b_lmm, freed(e))
                    nc.scalar.copy(xnT[:, e.u, :], bank[6 + e.u][:, 0:C]).then_inc(b_xnT, 1)
                if here:
                    act.wait_ge(b_gmm, done(s))
                    act.wait_ge(b_og, freed(s))
                    for f in range(NK):
                        last = nc.scalar.activation(sg[:, s.u, f * P:(f + 1) * P], bank[2 + s.u][:, P * (f + 1):P * (f + 2)],
                                                    ACT.Sigmoid, bias=vec[:, 2, f:f + 1])
                    last.then_inc(b_sg, 1)
                    act.wait_ge(b_alpha, done(s))
                    act.wait_ge(b_gn, freed(s))
                    nc.scalar.activation(sm[:, s.u, :], lg[:, s.u, HG:2 * HG], ACT.Exp, bias=lg[:, s.u, 2 * HG:2 * HG + 1],
                                         accum_out=lg[:, s.u, 2 * HG + 1:2 * HG + 2]).then_inc(b_exp, 1)
                if e:
                    act.wait_ge(b_lmm, done(e))
                    nc.scalar.copy(logits[:, ds(e.t * NE, NE)], bank[6 + e.u][:, C:C + NE]).then_inc(b_lc, 1)

            sweep(act, 2, step_b)

            act.wait_ge(s_w1, 16)
            for u in range(2):
                act.wait_ge(b_out[u], 32 * (NT // 2 + 1))

            def fold(e):
                act.wait_ge(w_mm[1], e + 1)
                for k in range(NK):
                    last = nc.scalar.copy(lnb_b[:, k * P:(k + 1) * P],
                                          flnb_sb[:, ds(e + k * NE, 1)].to_broadcast([P, P]))
                last.then_inc(w_le, 1)
                for j in range(2):
                    act.wait_ge(w_mm[j], e + 2)
                    nc.scalar.copy(b1_all[:, ds(e * HID + j * HJ, HJ)], bank[4 + j][:, :]).then_inc(w_c[j], 1)
                for k in range(NK):
                    part = w1_all[:, ds(e * (NK * HID) + k * HID, HID)]
                    last = nc.scalar.activation(part, part, ACT.Copy, scale=flng_sb[:, ds(e + k * NE, 1)])
                last.then_inc(w_s, 1)

            with act.Fori(0, NE) as e:
                fold(e)
            act.wait_ge(s_diff, 1)
            nc.scalar.activation(tok[:, 4, :], tok[:, 3, :], ACT.Exp).then_inc(s_exp, 1)

            act.wait_ge(s_table, 1)

            def rowsT(t):
                act.wait_ge(f_x, t + 2)
                act.wait_ge(f_h[1], t + 1)
                nc.scalar.copy(xsT, bank[0][:, 0:C]).then_inc(f_xc, 1)

            def gelu(t, j):
                act.wait_ge(f_hb[j], t + 2)
                act.wait_ge(f_t[j], t + 1)
                nc.scalar.activation(hid[:, j * HJ:(j + 1) * HJ], hpre[:, j * HJ:(j + 1) * HJ], ACT.Gelu
                                     ).then_inc(f_ge[j], 1)

            def hiddenT(t):
                act.wait_ge(f_t[1], t + 2)
                act.wait_ge(f_y[1], t + 1)
                nc.scalar.copy(hidT[:, HJ:2 * HJ], bank[7][:, :]).then_inc(f_tc[1], 1)

            rowsT(0)
            gelu(0, 0)
            gelu(0, 1)
            rowsT(1)
            with act.Fori(1, FT - 1) as t:
                hiddenT(t - 1)
                gelu(t, 0)
                gelu(t, 1)
                rowsT(t + 1)
            hiddenT(FT - 2)
            gelu(FT - 1, 0)
            gelu(FT - 1, 1)
            hiddenT(FT - 1)

        @block.vector
        def _(dve):
            chained = [0]

            def link(ins):
                chained[0] += 1
                ins.then_inc(s_r, 1)
                dve.wait_ge(s_r, chained[0])

            dve.wait_ge(s_w, 17 * 16)
            dve.wait_ge(s_pool, 18)
            for k in range(NK):
                for s in range(2):
                    link(nc.vector.tensor_tensor(x2[:, 0, :], wm[:, k, C:2 * C], attn_sb[:, s, :], ALU.mult))
                    link(nc.vector.tensor_reduce(wm[:, k, 2 * C + s * HG:2 * C + (s + 1) * HG],
                                                 x2[:, 0, :].rearrange("p (h d) -> p h d", h=HG), AX.X, ALU.add))
            for k in range(NK):
                nc.vector.tensor_copy(R3[:, 512 + k * P:512 + (k + 1) * P],
                                      vec[:, 1, k:k + 1].to_broadcast([P, P])).then_inc(s_lnb, 1)
            dve.wait_ge(s_bg, 1)
            nc.vector.tensor_tensor(bg1_sb[:, :], bg1_sb[:, :], bank[0][:, 0:GH], ALU.add).then_inc(s_prep, 1)
            for k in range(NK):
                nc.vector.tensor_scalar(wm[:, k, C + ROW:WM], wm[:, k, C + ROW:WM], vec[:, 0, k:k + 1], None,
                                        ALU.mult).then_inc(s_prep, 1)
            dve.wait_ge(s_prep, 1 + NK)

            def stats_a(s):
                u = s.u
                dve.wait_ge(a_in[u], landed(s))
                nc.vector.bn_stats(st[:, u, :], x_sb[:, u, :]).then_inc(a_stats, 1)
                dve.wait_ge(a_stats, done(s))
                dve.wait_ge(a_pow, freed(s))
                dve.sem_inc(s_held[0], 1)
                nc.vector.bn_aggr(mv[:, u, :], st[:, u, :]).then_inc(a_mv, 1)

            def norm_a(s):
                u = s.u
                dve.wait_ge(a_pow, done(s))
                dve.wait_ge(a_tr, freed(s))
                nc.vector.tensor_scalar(xn[:, u, :], x_sb[:, u, :], mv[:, u, 0:1], rs[:, u, 0:1],
                                        ALU.subtract, ALU.mult).then_inc(a_xn, 1)

            def take_a(s):
                u = s.u
                dve.wait_ge(a_kc, done(s))
                nc.vector.tensor_reduce(kmax[:, :, ds(s.t, 1)],
                                        kT_all.rearrange("p (k n) -> p k n", k=NK)[:, :, ds(s.t * P, P)], AX.X, ALU.max)
                dve.wait_ge(a_gmm, done(s))
                dve.wait_ge(a_tab[u], left(s, 32))
                nc.vector.tensor_copy(xt_sb[:, u, :], bank[6 + u][:, 0:ROW]).then_inc(a_row, 1)
                dve.wait_ge(a_gelu, freed(s))
                dve.wait_ge(a_r2, done(s))
                nc.vector.scalar_tensor_tensor(out=hgpre[:, u, :], in0=bank[6 + u][:, ROW:ROW + GH], scalar=r2[:, u, :],
                                               in1=bg1_sb[:, :], op0=ALU.mult, op1=ALU.add).then_inc(a_hg, 1)

            def step_a(s):
                if e := back(s, 1):
                    norm_a(e)
                if back(s, 0):
                    stats_a(s)
                if e := back(s, 2):
                    take_a(e)

            sweep(dve, 2, step_a)
            kv = kT_all.rearrange("p (k n) -> p k n", k=NK)
            nc.vector.tensor_reduce(kmax[:, :, LAST:LAST + 1], kv[:, :, LAST * P:N], AX.X, ALU.max).then_inc(s_kmax, 1)
            dve.wait_ge(s_kmax, 1)
            nc.vector.tensor_reduce(nkmax[:, :], kmax[:, :, 0:LAST + 1], AX.X, ALU.max, negate=True).then_inc(s_kmax, 1)
            nc.vector.memset(kv[:, :, N:NP], -1e30).then_inc(s_kmax, 1)

            def step_k(s):
                dve.wait_ge(k_tr, done(s))
                dve.wait_ge(k_mm, freed(s))
                nc.vector.tensor_copy(ekT[:, s.u, :], bank[s.u][:, 0:C]).then_inc(k_cp, 1)

            sweep(dve, 0, step_k)
            dve.wait_ge(k_exp, NT + 2)
            link(nc.vector.tensor_reduce(kinv[:, 0, :], ksum[:, :].rearrange("p (k n) -> p k n", k=NK), AX.X, ALU.add))
            link(nc.vector.reciprocal(kinv[:, 1, :], kinv[:, 0, :]))
            dve.wait_ge(s_csum, 1)
            for f in range(NK):
                for h in range(P // DM):
                    r = slice(h * DM, (h + 1) * DM)
                    ins = nc.vector.tensor_scalar(ctx_bd[r, f, r], bank[2 + f][r, r], kinv[r, 1, f:f + 1], None, ALU.mult)
            ins.then_inc(s_ctx, 1)

            def x2_b(s):
                u = s.u
                dve.wait_ge(b_pmm, done(s))
                dve.wait_ge(b_xb, done(s))
                nc.vector.tensor_tensor(x_sb[:, u, :], bank[4 + u][:, 0:C], x_sb[:, u, :], ALU.add).then_inc(b_mix, 1)
                dve.wait_ge(b_mix, done(s))
                dve.wait_ge(b_out[u], left(s, 32))
                dve.wait_ge(b_gn, done(s))
                nc.vector.scalar_tensor_tensor(out=x2[:, u, :].rearrange("p (h d) -> p h d", h=HG),
                                               in0=tmp[:, u, :].unsqueeze(1).to_broadcast([P, HG, DG]),
                                               scalar=lg[:, u, 10:11],
                                               in1=x_sb[:, u, :].rearrange("p (h d) -> p h d", h=HG),
                                               op0=ALU.mult, op1=ALU.add).then_inc(b_x2, 1)
                dve.wait_ge(b_x2, done(s))
                nc.vector.bn_stats(st[:, u, :], x2[:, u, :]).then_inc(b_stats, 1)
                dve.wait_ge(b_stats, done(s))
                dve.wait_ge(b_rstd, freed(s))
                dve.sem_inc(s_held[0], 1)
                nc.vector.bn_aggr(mv[:, u, :], st[:, u, :]).then_inc(b_mv, 1)

            def alpha_b(s):
                u = s.u
                dve.wait_ge(b_gat[u], s.i * 32 + 32)
                dve.wait_ge(b_exp, freed(s))
                nc.vector.tensor_tensor(lg[:, u, 0:HG], g2[:, u, :], xt_sb[:, u, C + HG:ROW], ALU.add).then_inc(b_al, 1)
                dve.wait_ge(b_al, done(s))
                nc.vector.scalar_tensor_tensor(out=lg[:, u, HG:2 * HG], in0=lg[:, u, 0:HG], scalar=0.01,
                                               in1=lg[:, u, 0:HG], op0=ALU.mult, op1=ALU.max).then_inc(b_lk, 1)
                dve.wait_ge(b_lk, done(s))
                nc.vector.tensor_reduce(lg[:, u, 8:9], lg[:, u, HG:2 * HG], AX.X, ALU.max, negate=True
                                        ).then_inc(b_alpha, 1)

            def gate_b(s):
                u = s.u
                dve.wait_ge(b_omm, done(s))
                dve.wait_ge(b_sg, done(s))
                dve.wait_ge(b_pmm, freed(s))
                nc.vector.tensor_tensor(og[:, u, :], bank[u][:, 0:C], sg[:, u, :], ALU.mult).then_inc(b_og, 1)

            def heads_b(s):
                u = s.u
                dve.wait_ge(b_exp, done(s))
                nc.vector.reciprocal(lg[:, u, 10:11], lg[:, u, 9:10])
                nc.vector.tensor_scalar(tmp[:, u, :], xt_sb[:, u, 0:DG], sm[:, u, 0:1], None, ALU.mult).then_inc(b_g0, 1)
                for h, (before, after) in enumerate(((b_g0, b_g1), (b_g1, b_g2), (b_g2, b_gn)), start=1):
                    dve.wait_ge(before, done(s))
                    nc.vector.scalar_tensor_tensor(out=tmp[:, u, :], in0=xt_sb[:, u, h * DG:(h + 1) * DG],
                                                   scalar=sm[:, u, h:h + 1], in1=tmp[:, u, :],
                                                   op0=ALU.mult, op1=ALU.add).then_inc(after, 1)

            def norm_b(s):
                u = s.u
                dve.wait_ge(b_rstd, done(s))
                dve.wait_ge(b_tr, freed(s))
                nc.vector.tensor_scalar(xn[:, u, :], x2[:, u, :], mv[:, u, 0:1], rs[:, u, 0:1],
                                        ALU.subtract, ALU.mult).then_inc(b_x3, 1)
                nc.vector.tensor_scalar(x4[:, u, :], x2[:, u, :], mv[:, u, 0:1], rs[:, u, 1:2],
                                        ALU.subtract, ALU.mult).then_inc(b_x4, 1)

            def step_b(s):
                if e := back(s, 1):
                    x2_b(e)
                if e := back(s, 0):
                    alpha_b(e)
                    gate_b(e)
                    heads_b(e)
                if e := back(s, 1):
                    norm_b(e)

            sweep(dve, 1, step_b)

            dve.wait_ge(b_lc, NT + 2)
            dve.wait_ge(s_pool, 19)
            for u in range(2):
                dve.wait_ge(b_out[u], 32 * (NT // 2 + 1))
            te3 = lambda a: a.rearrange("p (t e) -> p t e", e=NE)
            wide = lambda a: a.unsqueeze(2).to_broadcast([P, NT, NE])
            desc3 = desc[:, :].unsqueeze(1).to_broadcast([P, NT, NE])
            TOK, M, D, DIFF, EXP, W, SLOT = 0, 1, 2, 3, 4, 5, 7
            link(nc.vector.tensor_tensor(te3(logits), te3(logits), br_sb[:, :].unsqueeze(1).to_broadcast([P, NT, NE]), ALU.add))
            for k in range(2):
                of = work if k else logits
                m, d = tok[:, 9 + k, :], tok[:, D, :]
                link(nc.vector.tensor_reduce(m, te3(of), AX.X, ALU.max))
                link(nc.vector.tensor_tensor(te3(chosen), te3(of), wide(m), ALU.is_equal))
                link(nc.vector.tensor_tensor(te3(chosen), te3(chosen), desc3, ALU.mult))
                link(nc.vector.tensor_reduce(d, te3(chosen), AX.X, ALU.max))
                link(nc.vector.tensor_tensor(te3(oh[k]), desc3, wide(d), ALU.is_equal))
                if k == 0:
                    link(nc.vector.scalar_tensor_tensor(out=work, in0=oh[0], scalar=-BIG, in1=logits,
                                                        op0=ALU.mult, op1=ALU.add))
            link(nc.vector.tensor_scalar(tok[:, M, :], tok[:, TOK, :], float(N), None, ALU.is_lt))
            link(nc.vector.tensor_tensor(chosen, oh[0], oh[1], ALU.add))
            link(nc.vector.tensor_tensor(te3(chosen), te3(chosen), wide(tok[:, M, :]), ALU.mult))
            nc.vector.tensor_tensor(tok[:, DIFF, :], tok[:, 10, :], tok[:, 9, :], ALU.subtract).then_inc(s_diff, 1)
            dve.sem_inc(s_chosen, 1)
            dve.wait_ge(s_exp, 1)
            link(nc.vector.tensor_scalar(tok[:, D, :], tok[:, EXP, :], 1.0, None, ALU.add))
            link(nc.vector.reciprocal(tok[:, W, :], tok[:, D, :]))
            link(nc.vector.tensor_tensor(tok[:, W + 1, :], tok[:, EXP, :], tok[:, W, :], ALU.mult))
            dve.wait_ge(s_tot, 1)
            nc.vector.tensor_copy(ttb[0:NT, :].rearrange("p (e c) -> p e c", e=NE),
                                  bank[0][0:NT, 0:NE].unsqueeze(2).to_broadcast([NT, NE, P])).then_inc(s_ttb, 1)
            dve.wait_ge(s_pos, 1)
            link(nc.vector.tensor_copy(pos, bank[1][:, 0:NE * (NT + 1)]))
            pos3 = pos.rearrange("p (e t) -> p e t", e=NE)
            nc_e, size, base, end = (small[:, j, :] for j in range(4))
            link(nc.vector.tensor_scalar(small_i[:, 0, :], pos3[:, :, NT], float(P - 1), None, ALU.add))
            link(nc.vector.tensor_scalar(small_i[:, 1, :], small_i[:, 0, :], -P, None, ALU.bitwise_and))
            link(nc.vector.tensor_copy(size, small_i[:, 1, :]))
            link(nc.vector.memset(base[:, 0:1], 0.0))
            for e in range(NE):
                link(nc.vector.tensor_tensor(end[:, e:e + 1], base[:, e:e + 1], size[:, e:e + 1], ALU.add))
                if e + 1 < NE:
                    link(nc.vector.tensor_copy(base[:, e + 1:e + 2], end[:, e:e + 1]))
            link(nc.vector.tensor_scalar(sl[:, 0, :], cols[:, 0:FT], float(P), None, ALU.mult))
            link(nc.vector.tensor_scalar(sl[:, 1, :], sl[:, 0, :], end[:, 0:1], None, ALU.is_ge))
            for e in range(1, NE - 1):
                link(nc.vector.scalar_tensor_tensor(out=sl[:, 1, :], in0=sl[:, 0, :], scalar=end[:, e:e + 1],
                                                    in1=sl[:, 1, :], op0=ALU.is_ge, op1=ALU.add))
            link(nc.vector.tensor_copy(te, sl[0:1, 1, :]))
            pos_te = pos3[:, :, 0:NT]
            link(nc.vector.tensor_tensor(pos_te, pos_te, base.unsqueeze(2).to_broadcast([P, NE, NT]), ALU.add))
            link(nc.vector.tensor_scalar(tok[:, D, :], tok[:, M, :], -1000.0, 1000.0, ALU.mult, ALU.add))
            for k in range(2):
                slot = tok[:, SLOT + k, :]
                link(nc.vector.tensor_tensor(te3(work), te3(oh[k]), pos_te.rearrange("p e t -> p t e"), ALU.mult))
                link(nc.vector.tensor_reduce(slot, te3(work), AX.X, ALU.add))
                si, lo, hi = (tok_i[:, 3 * k + j, :] for j in range(3))
                link(nc.vector.tensor_copy(si, slot))
                link(nc.vector.tensor_scalar(lo, si, P - 1, None, ALU.bitwise_and))
                link(nc.vector.tensor_scalar(hi, si, 7, None, ALU.logical_shift_right))
                link(nc.vector.tensor_copy(tok[:, 11 + 2 * k, :], lo))
                link(nc.vector.tensor_tensor(tok[:, 11 + 2 * k, :], tok[:, 11 + 2 * k, :], tok[:, D, :], ALU.add))
                link(nc.vector.tensor_copy(tok[:, 12 + 2 * k, :], hi))
            link(nc.vector.tensor_scalar(tok[:, DIFF, :], tok[:, TOK, :], 1.0, None, ALU.add))

            def onehots(t):
                for k in range(2):
                    s = 2 * t + k
                    dve.wait_ge(t_mm, s + 1)
                    nc.vector.tensor_scalar(ohb[:, k, :], cols[:, :], tok[:, 11 + 2 * k, ds(t, 1)], None,
                                            ALU.is_equal).then_inc(t_oh, 1)
                    nc.vector.tensor_scalar(rv[:, k, 0:FT], cols[:, 0:FT], tok[:, 12 + 2 * k, ds(t, 1)],
                                            tok[:, DIFF, ds(t, 1)], ALU.is_equal, ALU.mult).then_inc(t_idx, 1)
                    nc.vector.tensor_scalar(rv[:, k, FT:2 * FT], cols[:, 0:FT], tok[:, 12 + 2 * k, ds(t, 1)],
                                            tok[:, W + k, ds(t, 1)], ALU.is_equal, ALU.mult).then_inc(t_w, 1)

            with dve.Fori(0, NT) as t:
                onehots(t)
            dve.wait_ge(s_table, 1)
            link(nc.vector.tensor_scalar(sl[:, 0, :], bank[2][:, 0:FT], 1.0, None, ALU.subtract))
            link(nc.vector.tensor_copy(slot_w, bank[2][:, FT:2 * FT]))
            link(nc.vector.tensor_scalar(gidx, sl[:, 0, :], 0.0, None, ALU.max))
            link(nc.vector.tensor_scalar(sl[:, 1, :], sl[:, 0, :], 0.0, None, ALU.is_lt))
            nc.vector.scalar_tensor_tensor(out=sidx, in0=sl[:, 1, :], scalar=dummy[:, 0:1], in1=sl[:, 0, :],
                                           op0=ALU.mult, op1=ALU.add).then_inc(s_slots, 1)

            dve.wait_ge(w_c[1], NE + 1)
            dve.wait_ge(s_b2, 16)

            def bias(t, e):
                for j in range(2):
                    dve.wait_ge(f_h[j], t + 2)
                    dve.wait_ge(f_ge[j], t + 1)
                    nc.vector.tensor_tensor(hpre[:, j * HJ:(j + 1) * HJ], bank[4 + j][:, :],
                                            b1_all[:, ds(e * HID + j * HJ, HJ)], ALU.add).then_inc(f_hb[j], 1)

            def hiddenT(t):
                dve.wait_ge(f_t[0], t + 2)
                dve.wait_ge(f_y[0], t + 1)
                nc.vector.tensor_copy(hidT[:, 0:HJ], bank[6][:, :]).then_inc(f_tc[0], 1)

            def rows(t, e):
                dve.wait_ge(f_y[1], t + 2)
                dve.wait_ge(f_yw, t + 1)
                nc.vector.tensor_tensor(y1, bank[1][:, 0:C], b2_all[:, ds(e * C, C)], ALU.add).then_inc(f_y1, 1)
                dve.wait_ge(f_y1, t + 2)
                if not (isinstance(t, int) and t == 0):
                    dve.wait_ge(f_add, 16 * t)
                nc.vector.tensor_scalar(yw, y1, slot_w[:, ds(t, 1)], None, ALU.mult).then_inc(f_yw, 1)

            def expert(t):
                return dve.value_load(te[0:1, ds(t, 1)], min_val=0, max_val=NE - 1)

            bias(0, expert(0))
            hiddenT(0)
            bias(1, expert(1))
            hiddenT(1)
            rows(0, expert(0))
            with dve.Fori(2, FT) as t:
                bias(t, expert(t))
                hiddenT(t)
                rows(t - 1, expert(t - 1))
            rows(FT - 1, expert(FT - 1))

        @block.tensor
        def _(pe):
            pe.wait_ge(s_lnb, NK)
            for k in range(NK):
                mm = nc.tensor.matmul(bank[0][:, 0:GH], R3[:, 512 + k * P:512 + (k + 1) * P], wm[:, k, C + ROW:WM],
                                      start=(k == 0), stop=(k == NK - 1))
            mm.then_inc(s_bg, 1)
            pe.wait_ge(s_prep, 1 + NK)

            def turn(out, src, s_out):
                for k in range(NK):
                    mm = nc.tensor.transpose(out[:, k * P:(k + 1) * P], src[:, k * P:(k + 1) * P], ident[:, :])
                mm.then_inc(s_out, 1)

            def project_a(s):
                u = s.u
                pe.wait_ge(a_xnT, done(s))
                pe.wait_ge(a_kc, freed(s))
                for f in range(NK):
                    for k in range(NK):
                        mm = nc.tensor.matmul(bank[2 + u][:, f * P:(f + 1) * P], wk_sb[:, k, f * P:(f + 1) * P],
                                              xnT[:, u, k * P:(k + 1) * P], start=(k == 0), stop=(k == NK - 1))
                mm.then_inc(a_kmm, 1)
                pe.wait_ge(a_vc, freed(s))
                for k in range(NK):
                    mm = nc.tensor.matmul(bank[4 + u][:, 0:C], xnT[:, u, k * P:(k + 1) * P], wm[:, k, 0:C],
                                          start=(k == 0), stop=(k == NK - 1))
                mm.then_inc(a_vmm, 1)
                pe.wait_ge(a_hg, freed(s))
                for k in range(NK):
                    mm = nc.tensor.matmul(bank[6 + u][:, 0:ROW + GH], xnT[:, u, k * P:(k + 1) * P], wm[:, k, C:WM],
                                          start=(k == 0), stop=(k == NK - 1))
                mm.then_inc(a_gmm, 1)

            def step_a(s):
                if e := back(s, 0):
                    pe.wait_ge(a_xn, done(e))
                    pe.wait_ge(a_xnT, freed(e))
                    turn(bank[e.u], xn[:, e.u, :], a_tr)
                if e := back(s, 1):
                    project_a(e)

            sweep(pe, 1, step_a)

            def zeros(outs, **flags):
                for o in outs:
                    mm = nc.tensor.matmul(o, zrow[:, 0:P], zrow[:, 0:o.shape[1]], **flags)
                return mm

            def step_k(s):
                if e := back(s, 0):
                    pe.wait_ge(k_exp, done(e))
                    pe.wait_ge(k_cp, freed(e))
                    turn(bank[e.u], ek[:, e.u, :], k_tr)
                if e := back(s, 1):
                    pe.wait_ge(k_cp, done(e))
                    for f in range(NK):
                        mm = nc.tensor.matmul(bank[2 + f][:, 0:P], ekT[:, e.u, f * P:(f + 1) * P],
                                              v_all[:, ds(e.t * C + f * P, P)], start=False, stop=False)
                    mm.then_inc(k_mm, 1)

            pe.wait_ge(a_kc, NT + 2)
            sums = [bank[2][:, 0:P], bank[3][:, 0:P]]
            zeros(sums, start=True, stop=False)
            sweep(pe, 1, step_k)
            zeros(sums, start=False, stop=True).then_inc(s_csum, 1)
            pe.wait_ge(s_ctx, 1)
            for k in range(NK):
                for f in range(NK):
                    mm = nc.tensor.matmul(bank[4][:, k * C + f * P:k * C + (f + 1) * P], wqT_sb[:, f, k * P:(k + 1) * P],
                                          ctx_bd[:, f, :], start=True, stop=True)
            mm.then_inc(s_m1, 1)
            pe.wait_ge(s_m1c, 1)

            def step_b(s):
                here, before, old = back(s, 0), back(s, 1), back(s, 2)
                if here:
                    u = here.u
                    pe.wait_ge(b_og, freed(here))
                    for f in range(NK):
                        for k in range(NK):
                            mm = nc.tensor.matmul(bank[u][:, f * P:(f + 1) * P], m1[:, k, f * P:(f + 1) * P],
                                                  tile_of(xnT_all, k, here), start=(k == 0), stop=(k == NK - 1))
                    mm.then_inc(b_omm, 1)
                    pe.wait_ge(b_hgb, done(here))
                    pe.wait_ge(b_sg, freed(here))
                    pe.sem_inc(s_held[1], 1)
                    nc.tensor.transpose(bank[2 + u][0:GH, 0:P], hgb[:, u, :], ident[:, :]).then_inc(b_htr, 1)
                if old:
                    pe.wait_ge(b_x3, done(old))
                    pe.wait_ge(b_lc, freed(old))
                    turn(bank[6 + old.u], xn[:, old.u, :], b_tr)
                if before:
                    u = before.u
                    pe.wait_ge(b_og, done(before))
                    pe.wait_ge(b_mix, freed(before))
                    for f in range(NK):
                        mm = nc.tensor.matmul(bank[4 + u][:, 0:C], og[:, u, f * P:(f + 1) * P], wproj_sb[:, f, :],
                                              start=(f == 0), stop=(f == NK - 1))
                    mm.then_inc(b_pmm, 1)
                if here:
                    u = here.u
                    pe.wait_ge(b_hgT, done(here))
                    for f in range(NK):
                        mm = nc.tensor.matmul(bank[2 + u][:, (f + 1) * P:(f + 2) * P], wg2_sb[:, f * P:(f + 1) * P],
                                              hgT[0:GH, u, :], start=True, stop=True)
                    mm.then_inc(b_gmm, 1)
                if old:
                    u = old.u
                    pe.wait_ge(b_xnT, done(old))
                    for k in range(NK):
                        mm = nc.tensor.matmul(bank[6 + u][:, C:C + NE], xnT[:, u, k * P:(k + 1) * P], wr_sb[:, k, :],
                                              start=(k == 0), stop=(k == NK - 1))
                    mm.then_inc(b_lmm, 1)

            sweep(pe, 2, step_b)

            pe.wait_ge(s_b1, 16)

            def biases(e):
                pe.wait_ge(w_le, e + 2)
                for j in range(2):
                    pe.wait_ge(w_c[j], e + 1)
                    nc.tensor.matmul(bank[4 + j][:, :], ones[0:1, :], b1_all[0:1, ds(e * HID + j * HJ, HJ)],
                                     start=True, stop=False)
                    for k in range(NK):
                        mm = nc.tensor.matmul(bank[4 + j][:, :], lnb_b[:, k * P:(k + 1) * P],
                                              w1_all[:, ds(e * (NK * HID) + k * HID + j * HJ, HJ)],
                                              start=False, stop=(k == NK - 1))
                    mm.then_inc(w_mm[j], 1)

            with pe.Fori(0, NE) as e:
                biases(e)

            pe.wait_ge(s_chosen, 1)
            ch3 = chosen.rearrange("p (t e) -> p t e", e=NE)
            for e in range(NE):
                mm = nc.tensor.matmul(bank[0][0:NT, e:e + 1], ch3[:, :, e], ones[:, 0:1], start=True, stop=True)
            mm.then_inc(s_tot, 1)
            pe.wait_ge(s_ttb, 1)
            for e in range(NE):
                at = e * (NT + 1)
                nc.tensor.matmul(bank[1][:, at:at + NT + 1], ttb[0:NT, e * P:(e + 1) * P], upper[0:NT, 0:NT + 1],
                                 start=True, stop=False)
                mm = nc.tensor.matmul(bank[1][:, at:at + NT], upper[:, :], ch3[:, :, e], start=False, stop=True)
            mm.then_inc(s_pos, 1)
            table = bank[2][:, 0:2 * FT]
            zeros([table], start=True, stop=False)
            with pe.Fori(0, NT) as t:
                for k in range(2):
                    s = 2 * t + k
                    pe.wait_ge(t_oh, s + 3)
                    pe.wait_ge(t_idx, s + 3)
                    pe.wait_ge(t_w, s + 3)
                    nc.tensor.matmul(table, ohb[:, k, :], rv[:, k, :], start=False, stop=False).then_inc(t_mm, 1)
            zeros([table], start=False, stop=True).then_inc(s_table, 1)

            def expert(t):
                return pe.value_load(te[0:1, ds(t, 1)], min_val=0, max_val=NE - 1)

            def rows(t):
                pe.wait_ge(f_gat, 16 * t + 16)
                pe.wait_ge(f_xc, t + 1)
                turn(bank[0], xs, f_x)

            def hidden(t, e, j):
                pe.wait_ge(f_xc, t + 2)
                pe.wait_ge(f_hb[j], t + 1)
                for k in range(NK):
                    mm = nc.tensor.matmul(bank[4 + j][:, :], xsT[:, k * P:(k + 1) * P],
                                          w1_all[:, ds(e * (NK * HID) + k * HID + j * HJ, HJ)],
                                          start=(k == 0), stop=(k == NK - 1))
                mm.then_inc(f_h[j], 1)

            def hidden_turn(t, j):
                pe.wait_ge(f_ge[j], t + 2)
                pe.wait_ge(f_tc[j], t + 1)
                for c in range(HC):
                    mm = nc.tensor.transpose(bank[6 + j][:, c * P:(c + 1) * P],
                                             hid[:, j * HJ + c * P:j * HJ + (c + 1) * P], ident[:, :])
                mm.then_inc(f_t[j], 1)

            def second(t, e, j):
                pe.wait_ge(f_tc[j], t + 2)
                if j == 0:
                    pe.wait_ge(f_y1, t + 1)
                for c in range(HC):
                    mm = nc.tensor.matmul(bank[1][:, 0:C], hidT[:, j * HJ + c * P:j * HJ + (c + 1) * P],
                                          w2_all[:, ds(e * (2 * HC * C) + (j * HC + c) * C, C)],
                                          start=(j == 0 and c == 0), stop=(j == 1 and c == HC - 1))
                mm.then_inc(f_y[j], 1)

            pe.wait_ge(w_s, NE + 1)
            pe.wait_ge(s_w2, 16)
            pe.wait_ge(s_slots, 1)
            rows(0)
            e = expert(0)
            hidden(0, e, 0)
            hidden(0, e, 1)
            rows(1)
            hidden_turn(0, 0)
            with pe.Fori(1, FT - 1) as t:
                now, last = expert(t), expert(t - 1)
                hidden(t, now, 0)
                hidden_turn(t - 1, 1)
                second(t - 1, last, 0)
                hidden(t, now, 1)
                rows(t + 1)
                hidden_turn(t, 0)
                second(t - 1, last, 1)
            now, last = expert(FT - 1), expert(FT - 2)
            hidden(FT - 1, now, 0)
            hidden_turn(FT - 2, 1)
            second(FT - 2, last, 0)
            hidden(FT - 1, now, 1)
            hidden_turn(FT - 1, 0)
            second(FT - 2, last, 1)
            hidden_turn(FT - 1, 1)
            second(FT - 1, now, 0)
            second(FT - 1, now, 1)


def kernel(x, src, dst, L0_gnn_weight, L0_gnn_attn_l, L0_gnn_attn_r, L0_mix_Wqkv, L0_mix_Wproj, L0_mix_bproj,
           L0_mix_ln_g, L0_mix_ln_b, L0_mix_Wg1, L0_mix_bg1, L0_mix_Wg2, L0_mix_bg2, L0_ffn_Wr, L0_ffn_br,
           L0_ffn_ln_g, L0_ffn_ln_b, L0_ffn_W1, L0_ffn_b1, L0_ffn_W2, L0_ffn_b2):
    import numpy as np
    import concourse.bacc as bacc
    from concourse.bass_utils import run_bass_kernel_spmd as run

    def chunks(w):
        w = np.asarray(w)
        return w.reshape(-1, P, w.shape[-1]).transpose(1, 0, 2)

    def rows(v):
        v = np.asarray(v).reshape(1, -1)
        return np.broadcast_to(v, (P, v.shape[1]))

    def columns(v):
        v = np.asarray(v)
        v = v.reshape(-1, NK, P).transpose(2, 1, 0)
        return v.reshape(P, -1)

    def tokens(a):
        padded = np.zeros(NP, np.asarray(a).dtype)
        padded[:N] = np.asarray(a)[:N]
        return padded.reshape(NT, P).T

    wqkv = np.asarray(L0_mix_Wqkv)
    xp = np.zeros((NP, C), np.float32)
    xp[:N] = np.asarray(x)
    attn = np.stack([np.asarray(L0_gnn_attn_l).reshape(-1), np.asarray(L0_gnn_attn_r).reshape(-1)])
    w1 = np.asarray(L0_ffn_W1).reshape(NE, NK, P, HID).transpose(2, 0, 1, 3).reshape(P, -1)
    w2 = np.asarray(L0_ffn_W2).reshape(NE, HID // P, P, C).transpose(2, 0, 1, 3).reshape(P, -1)
    vecs = np.stack([columns(v) for v in (L0_mix_ln_g, L0_mix_ln_b, L0_mix_bg2)], axis=1)
    arrays = {
        "x": xp, "src": tokens(src), "dst": tokens(dst),
        "wk": chunks(wqkv[:, C:2 * C]), "wqT": chunks(wqkv[:, 0:C].T), "wv": chunks(wqkv[:, 2 * C:3 * C]),
        "wgnn": chunks(L0_gnn_weight), "attn": np.broadcast_to(attn[None], (P, 2, C)),
        "wproj": chunks(L0_mix_Wproj), "bproj": rows(L0_mix_bproj), "vecs": vecs,
        "wg1": chunks(L0_mix_Wg1), "bg1": rows(L0_mix_bg1), "wg2": np.asarray(L0_mix_Wg2),
        "wr": chunks(L0_ffn_Wr), "br": rows(L0_ffn_br), "flng": columns(L0_ffn_ln_g), "flnb": columns(L0_ffn_ln_b),
        "w1": w1, "b1": np.asarray(L0_ffn_b1).reshape(1, -1), "w2": w2, "b2": rows(L0_ffn_b2),
    }
    arrays = {k: np.ascontiguousarray(a) for k, a in arrays.items()}
    nc = bacc.Bacc("TRN2", target_bir_lowering=False, num_devices=1)
    args = {k: nc.dram_tensor(k + "_in", a.shape, mybir.dt.from_np(a.dtype), kind="ExternalInput").ap()
            for k, a in arrays.items()}
    fp32 = mybir.dt.float32
    args["out"] = nc.dram_tensor("rows_out", (NP + P, C), fp32, kind="ExternalOutput").ap()
    for name, shape in (("xt_table", (NP, ROW)), ("al_table", (NP, HG)), ("x4_table", (NP, C))):
        args[name] = nc.dram_tensor(name, shape, fp32, kind="Internal").ap()
    gps_layer(nc, **args)
    r = run(nc, [{k + "_in": a for k, a in arrays.items()}], core_ids=[0])
    return np.asarray(r.results[0]["rows_out"])[:N]
```

```python
import concourse.bass as bass
from concourse import mybir
from contextlib import ExitStack
from collections import namedtuple

P = 128
N, C = 6250, 256
NT = 50
NP = NT * P
LAST = N // P
NK = C // P
HG, DG = 4, 64
DM = 32
GH = C // 4
NE, HID = 8, 1024
HJ = HID // 2
HC = HJ // P
FT = (2 * N + NE * (P - 1)) // P
ROW = C + 2 * HG
WM = C + ROW + GH
EPS = 1e-5
BIG = 3.0e38

Tile = namedtuple("Tile", "t u i")


def back(tile, lag):
    t, u = tile.t - lag, (tile.u - lag) % 2
    if isinstance(t, int) and not 0 <= t < NT:
        return None
    return Tile(t, u, tile.i + (tile.u - lag - u) // 2)


def sweep(eng, last_lag, step):
    lead = 2 * ((last_lag + 1) // 2)
    for s in range(lead):
        step(Tile(s, s % 2, s // 2))
    with eng.Fori(lead // 2, NT // 2) as i:
        for u in range(2):
            step(Tile(2 * i + u, u, i))
    for s in range(NT, NT + last_lag):
        step(Tile(s, s % 2, s // 2))


def done(tile):
    return tile.t + 3


def freed(tile):
    return tile.t + 1


def landed(tile, each=16):
    return tile.i * each + 2 * each


def left(tile, each=16):
    return tile.i * each + each


def gps_layer(nc, x, edges, wk, wqT, wv, wgnn, attn, wproj, bproj, vecs, wg1, bg1, wg2,
              wr, br, flng, flnb, w1, b1, w2, b2, out, xt_table, al_table, x4_table, xb_table):
    fp32, i32 = mybir.dt.float32, mybir.dt.int32
    ALU = mybir.AluOpType
    ACT = mybir.ActivationFunctionType
    AX = mybir.AxisListType
    ds = bass.ds

    with ExitStack() as ctx:
        def sb(name, shape, dt=fp32):
            return ctx.enter_context(nc.sbuf_tensor(name, shape, dt))

        R1 = sb("R1", [P, 2 * NK * NP])
        kT_all, v_all = R1[:, 0:NK * NP], R1[:, NK * NP:2 * NK * NP]
        w1_all = R1[:, 0:NE * NK * HID]
        b1_all = R1[:, NE * NK * HID:NE * (NK + 1) * HID]
        R2 = sb("R2", [P, NE * NK * HID])
        xnT_all, hg_all = R2[:, 0:NK * NP], R2[:, NK * NP:NK * NP + NT * GH]
        w2_all = R2
        RA = sb("RA", [P, NK * WM + NK * C + 2 * C])
        wm = RA[:, 0:NK * WM].rearrange("p (k c) -> p k c", k=NK)
        wk_sb = RA[:, NK * WM:NK * (WM + C)].rearrange("p (k c) -> p k c", k=NK)
        attn_sb = RA[:, NK * (WM + C):NK * (WM + C) + 2 * C].rearrange("p (s c) -> p s c", s=2)
        b2_all = RA[:, 0:NE * C]
        R3 = sb("R3", [P, 5120])

        def pair(at, width):
            return R3[:, at:at + 2 * width].rearrange("p (u c) -> p u c", u=2)

        x_sb, xn, xnT, xt_sb = pair(0, C), pair(512, C), pair(1024, C), pair(1536, ROW)
        sg, og, x2, x4 = pair(2064, C), pair(2576, C), pair(3088, C), pair(3600, C)
        tmp, hgT, hgb, hgpre = pair(4112, DG), pair(4240, P), pair(4496, GH), pair(4624, GH)
        ek, ekT = sg, og
        ttb = R3[:, 1024:1024 + NE * P]
        rv, ohb, far = (R3[:, a:a + 4 * w].rearrange("p (b c) -> p b c", b=4) for a, w in ((0, 2 * FT), (1050, P), (1562, FT)))
        xs, xsT = R3[:, 0:C], R3[:, C:2 * C]
        hpre, hid, hidT = R3[:, 512:512 + HID], R3[:, 1536:1536 + HID], R3[:, 2560:2560 + HID]
        y1, yw = R3[:, 3584:3584 + C], R3[:, 3840:3840 + C]
        wqT_sb, wproj_sb, m1 = (sb(n, [P, NK, C]) for n in ("wqT_sb", "wproj_sb", "m1"))
        wg2_sb = sb("wg2_sb", [GH, C])
        bproj_sb, bg1_sb, br_sb = sb("bproj_sb", [P, C]), sb("bg1_sb", [P, GH]), sb("br_sb", [P, NE])
        vec = sb("vec", [P, 3, NK])
        wr_sb = sb("wr_sb", [P, NK, NE])
        flng_sb, flnb_sb = sb("flng_sb", [P, NK * NE]), sb("flnb_sb", [P, NK * NE])
        ident, ones, upper = sb("ident", [P, P]), sb("ones", [P, P]), sb("upper", [P, P])
        cols = sb("cols", [P, P])
        ctx_bd = sb("ctx_bd", [P, NK, P])
        edges_i = sb("edges_i", [P, NT * 2], i32)
        idx = sb("idx", [P, 4], i32)
        st, mv = sb("st", [P, 2, 6]), sb("mv", [P, 2, 2])
        va, rs, r2 = (sb(n, [P, 2, w]) for n, w in (("va", 3), ("rs", 3), ("r2", 1)))
        cexp = sb("cexp", [P, 3])
        kmax, nkmax = sb("kmax", [P, NK, NT]), sb("nkmax", [P, NK])
        ksum, kinv = sb("ksum", [P, NK * NT]), sb("kinv", [P, 2, NK])
        g2, lg, sm = sb("g2", [P, 2, HG]), sb("lg", [P, 2, 3 * HG]), sb("sm", [P, 2, 4])
        TE = NT * NE
        logits = wqT_sb[:, :, :].rearrange("p k c -> p (k c)")[:, 0:TE]
        work, chosen, oh0, oh1 = (R3[:, 2048 + j * TE:2048 + (j + 1) * TE] for j in range(4))
        oh = [oh0, oh1]
        pos = R3[:, 2048 + 4 * TE:2048 + 5 * TE + NE]
        at = NE * (NK + 1) * HID
        tok = R1[:, at:at + 16 * NT].rearrange("p (j t) -> p j t", t=NT)
        tok_i = R3[:, 4352:4352 + 6 * NT].bitcast(i32).rearrange("p (j t) -> p j t", t=NT)
        gidx, sidx, slot_w, te = (R3[:, 4652 + j * FT:4652 + (j + 1) * FT] for j in range(4))
        gidx, sidx, te = gidx.bitcast(i32), sidx.bitcast(i32), te[0:1, :].bitcast(i32)
        sl = R3[:, 840:840 + 2 * FT].rearrange("p (j t) -> p j t", j=2)
        desc = sb("desc", [P, NE])
        small = sb("small", [P, 4, NE])
        small_i = sb("small_i", [P, 2, NE], i32)
        dummy = sb("dummy_row", [P, 1])
        zrow = sb("zrow", [P, C])
        bank = [ctx.enter_context(nc.psum_tensor(f"bank{b}", [P, 512], fp32)) for b in range(8)]

        at_start = {}

        def counts(prefix, names, start):
            made = [ctx.enter_context(nc.semaphore(f"{prefix}_{n}")) for n in names.split()]
            for s in made:
                at_start[id(s)] = (s, start)
            return made

        a_stats, a_mv, a_va, a_pow, a_r2, a_xn, a_tr, a_xnT, a_all, a_xb = counts(
            "a", "stats mv va pow r2 xn tr xnT all xb", 2)
        a_kmm, a_vmm, a_gmm, a_kc, a_vc, a_row, a_hg, a_gelu = counts(
            "a", "kmm vmm gmm kc vc row hg gelu", 2)
        k_exp, k_tr, k_cp, k_mm = counts("k", "exp tr cp mm", 2)
        b_omm, b_htr, b_hgT, b_gmm, b_sg, b_og, b_pmm = counts("b", "omm htr hgT gmm sg og pmm", 2)
        b_hgb, b_idx, b_al, b_lk, b_alpha, b_exp = counts("b", "hgb idx al lk alpha exp", 2)
        b_g0, b_g1, b_g2, b_gn, b_mix, b_x2, b_stats, b_mv = counts("b", "g0 g1 g2 gn mix x2 stats mv", 2)
        b_va, b_rstd, b_r2, b_x3, b_x4, b_tr, b_xnT, b_lmm, b_lc = counts(
            "b", "va rstd r2 x3 x4 tr xnT lmm lc", 2)
        t_oh, t_idx, t_far, t_w, t_mm = counts("t", "oh idx far w mm", 4)
        f_gi, f_si, f_x, f_xc, f_y1, f_yw = counts("f", "gi si x xc y1 yw", 1)
        f_h, f_hb, f_ge, f_t, f_tc, f_y = (counts("f", f"{n}0 {n}1", 1) for n in ("hmm", "hb", "ge", "tr", "tc", "ymm"))
        a_in, a_xbo, b_in = counts("a", "in0 in1", 16), counts("a", "xbo0 xbo1", 16), counts("b", "in0 in1", 16)
        a_tab = counts("a", "tab0 tab1", 32)
        b_x2o, b_x4o = counts("b", "x2o0 x2o1", 16), counts("b", "x4o0 x4o1", 16)
        b_gat, (f_gat, f_add) = counts("b", "gat0 gat1", 0), counts("f", "gat add", 0)
        (s_w, s_pool, s_half, s_lnb, s_bg, s_bgc, s_prep, s_kmax, s_csum, s_ctx, s_m1, s_m1c, s_w1, s_w2, s_b1, s_b2,
         s_r, s_chosen, s_tot, s_ttb, s_pos, s_diff, s_exp, s_low, s_table, s_slots, s_dummy) = counts(
            "s", "w pool half lnb bg bgc prep kmax csum ctx m1 m1c w1 w2 b1 b2 r chosen tot ttb pos diff exp low table slots dummy", 0)

        s_held = counts("s", "held_dve held_pe held_pool", 0)

        block = ctx.enter_context(nc.Block())
        x_t, out_t, xt_t, al_t, x4_t, xb_t = (a.rearrange("(t p) c -> t p c", p=P)
                                        for a in (x, out, xt_table, al_table, x4_table, xb_table))

        def tile_of(all_tokens, k, tile):
            return all_tokens[:, ds(tile.t * P + k * NP, P)]

        @block.sync
        def _(sp):
            for t, a in ((wm[:, :, 0:C], wv), (wm[:, :, C:2 * C], wgnn), (wm[:, :, C + ROW:WM], wg1),
                         (wk_sb, wk), (attn_sb, attn), (wqT_sb, wqT), (wproj_sb, wproj), (wg2_sb, wg2),
                         (bproj_sb, bproj), (bg1_sb, bg1), (br_sb, br), (vec, vecs), (wr_sb, wr),
                         (flng_sb, flng), (flnb_sb, flnb), (edges_i, edges)):
                sp.dma_start(t if isinstance(t, bass.AP) else t[:], a).then_inc(s_w, 16)

            def load_a(s):
                sp.lower_val(s.t), sp.lower_val(freed(s)), sp.lower_val(landed(s))
                if e := back(s, 0):
                    sp.wait_ge(a_xn, freed(e))
                    sp.wait_ge(a_xb, freed(e))
                    sp.dma_start(x_sb[:, e.u, :], x_t[e.t, :, :]).then_inc(a_in[e.u], 16)
                if e := back(s, 1):
                    sp.lower_val(done(e)), sp.lower_val(e.t)
                    sp.wait_ge(a_xb, done(e))
                    sp.dma_start(xb_t[e.t, :, :], x2[:, e.u, :]).then_inc(a_xbo[e.u], 16)

            sweep(sp, 1, load_a)
            def rows_b(s):
                sp.lower_val(s.t), sp.lower_val(freed(s)), sp.lower_val(s.i)
                if e := back(s, 0):
                    sp.wait_ge(b_x2, freed(e))
                    sp.dma_start(x_sb[:, e.u, :], xb_t[e.t, :, :]).then_inc(b_in[e.u], 16)
                if e := back(s, 2):
                    sp.lower_val(done(e)), sp.lower_val(e.t)
                    sp.wait_ge(b_x2, done(e))
                    sp.dma_start(out_t[e.t, :, :], x2[:, e.u, :]).then_inc(b_x2o[e.u], 16)
                if e := back(s, 5):
                    sp.lower_val(done(e)), sp.lower_val(e.t)
                    sp.wait_ge(b_x4, done(e))
                    sp.dma_start(x4_t[e.t, :, :], x4[:, e.u, :]).then_inc(b_x4o[e.u], 16)

            sp.wait_ge(a_xn, NT + 2)
            for u in range(2):
                sp.wait_ge(a_xbo[u], 16 * (NT // 2 + 1))
            sweep(sp, 5, rows_b)
            sp.wait_ge(s_ctx, 1)
            sp.dma_start(w1_all, w1).then_inc(s_w1, 16)
            sp.dma_start(b2_all, b2).then_inc(s_b2, 16)
            sp.wait_ge(b_omm, NT + 2)
            sp.wait_ge(b_hgb, NT + 2)
            sp.dma_start(w2_all[:, :], w2).then_inc(s_w2, 16)
            sp.dma_start(b1_all, b1.to_broadcast([P, NE * HID])).then_inc(s_b1, 16)
            sp.dma_start(out[NP:NP + P, :], zrow[:, :]).then_inc(s_dummy, 16)
            sp.wait_ge(s_dummy, 16)
            sp.wait_ge(f_add, 16 * FT)
            for u in range(2):
                sp.wait_ge(b_x2o[u], 16 * (NT // 2 + 1))
                sp.wait_ge(b_x4o[u], 16 * (NT // 2 + 1))

        @block.gpsimd
        def _(pool):
            for s, start in at_start.values():
                if start:
                    pool.sem_inc(s, start)
            nc.gpsimd.memset(ones[:, :], 1.0).then_inc(s_pool, 1)
            nc.gpsimd.memset(ident[:, :], 0.0).then_inc(s_pool, 1)
            nc.gpsimd.iota(cols[:, :], pattern=[[1, P]], base=0, channel_multiplier=0,
                           allow_small_or_imprecise_dtypes=True).then_inc(s_pool, 1)
            nc.gpsimd.iota(desc[:, :], pattern=[[-1, NE]], base=NE, channel_multiplier=0,
                           allow_small_or_imprecise_dtypes=True).then_inc(s_pool, 1)
            nc.gpsimd.iota(dummy[:, :], pattern=[[0, 1]], base=NP + 1, channel_multiplier=1,
                           allow_small_or_imprecise_dtypes=True).then_inc(s_pool, 1)
            nc.gpsimd.memset(ctx_bd[:, :, :], 0.0).then_inc(s_pool, 1)
            nc.gpsimd.memset(zrow[:, :], 0.0).then_inc(s_pool, 1)
            for j, power_of in enumerate((-0.5, 0.5, -0.5)):
                nc.gpsimd.memset(cexp[:, j:j + 1], power_of).then_inc(s_pool, 1)
            pool.wait_ge(s_pool, 10)
            nc.gpsimd.affine_select(out=ident[:, :], in_=ident[:, :], compare_op=ALU.not_equal, fill=1.0, base=0,
                                    pattern=[[-1, P]], channel_multiplier=1).then_inc(s_pool, 1)
            nc.gpsimd.affine_select(out=upper[:, :], in_=ones[:, :], compare_op=ALU.is_gt, fill=0.0, base=0,
                                    pattern=[[1, P]], channel_multiplier=-1).then_inc(s_pool, 1)

            def power(s, va_sem, s_out, freed_by):
                pool.wait_ge(va_sem, done(s))
                pool.wait_ge(freed_by, freed(s))
                nc.gpsimd.tensor_tensor(rs[:, s.u, :], va[:, s.u, :], cexp[:, :], ALU.pow).then_inc(s_out, 1)

            def step_a(s):
                if back(s, 0):
                    pool.wait_ge(a_r2, freed(s))
                    power(s, a_va, a_pow, a_xn)
                if e := back(s, 1):
                    pool.wait_ge(a_pow, done(e))
                    pool.wait_ge(a_hg, freed(e))
                    nc.gpsimd.tensor_tensor(r2[:, e.u, :], rs[:, e.u, 1:2], rs[:, e.u, 2:3], ALU.mult).then_inc(a_r2, 1)
                if back(s, 0):
                    pool.wait_ge(a_in[s.u], landed(s))
                    pool.wait_ge(a_xbo[s.u], left(s))
                    nc.gpsimd.tensor_tensor(x2[:, s.u, :], x_sb[:, s.u, :], bproj_sb[:, :], ALU.add).then_inc(a_xb, 1)

            sweep(pool, 1, step_a)
            pool.wait_ge(s_ctx, 1)
            nc.gpsimd.iota(tok[:, 0, :], pattern=[[P, NT]], base=0, channel_multiplier=1,
                           allow_small_or_imprecise_dtypes=True).then_inc(s_pool, 1)
            pool.wait_ge(s_w, 16 * 16)
            for u in range(2):
                pool.wait_ge(a_tab[u], 32 * (NT // 2 + 1))

            def step_b(s):
                if e := back(s, 4):
                    power(e, b_va, b_rstd, b_r2)
                if back(s, 0):
                    u = s.u
                    pool.wait_ge(b_gn, freed(s))
                    nc.gpsimd.tensor_copy(idx[:, 2 * u:2 * u + 2], edges_i[:, ds(s.t * 2, 2)]).then_inc(b_idx, 1)
                    pool.wait_ge(b_idx, done(s))
                    pool.sem_inc(s_held[2], 1)
                    nc.gpsimd.indirect_dma_start(out=xt_sb[:, u, :], out_offset=None, in_=xt_table,
                                                 in_offset=bass.IndirectOffsetOnAxis(ap=idx[:, 2 * u:2 * u + 1], axis=0)
                                                 ).then_inc(b_gat[u], 16)
                    nc.gpsimd.indirect_dma_start(out=g2[:, u, :], out_offset=None, in_=al_table,
                                                 in_offset=bass.IndirectOffsetOnAxis(ap=idx[:, 2 * u + 1:2 * u + 2], axis=0)
                                                 ).then_inc(b_gat[u], 16)

            sweep(pool, 4, step_b)

            pool.wait_ge(s_slots, 1)
            for u in range(2):
                pool.wait_ge(b_x2o[u], 16 * (NT // 2 + 1))
                pool.wait_ge(b_x4o[u], 16 * (NT // 2 + 1))
            pool.wait_ge(s_dummy, 16)

            def gather(t):
                pool.wait_ge(f_x, t + 1)
                nc.gpsimd.tensor_copy(idx[:, 0:1], gidx[:, ds(t, 1)]).then_inc(f_gi, 1)
                pool.wait_ge(f_gi, t + 2)
                pool.sem_inc(s_held[2], 1)
                nc.gpsimd.indirect_dma_start(out=xs, out_offset=None, in_=x4_table,
                                             in_offset=bass.IndirectOffsetOnAxis(ap=idx[:, 0:1], axis=0)
                                             ).then_inc(f_gat, 16)

            def add(t):
                if not (isinstance(t, int) and t == 0):
                    pool.wait_ge(f_add, 16 * t)
                nc.gpsimd.tensor_copy(idx[:, 1:2], sidx[:, ds(t, 1)]).then_inc(f_si, 1)
                pool.wait_ge(f_si, t + 2)
                pool.wait_ge(f_yw, t + 2)
                pool.sem_inc(s_held[2], 1)
                nc.gpsimd.indirect_dma_start(out=out, out_offset=bass.IndirectOffsetOnAxis(ap=idx[:, 1:2], axis=0),
                                             in_=yw, in_offset=None, compute_op=ALU.add).then_inc(f_add, 16)

            for t in range(3):
                gather(t)
            add(0)
            with pool.Fori(3, FT) as t:
                gather(t)
                add(t - 2)
            add(FT - 2)
            add(FT - 1)

        @block.scalar
        def _(act):
            def step_a(s):
                if back(s, 0):
                    act.wait_ge(a_tr, done(s))
                    act.wait_ge(a_gmm, freed(s))
                    nc.scalar.copy(xnT[:, s.u, :], bank[s.u][:, 0:C]).then_inc(a_xnT, 1)
                if e := back(s, 1):
                    u = e.u
                    act.wait_ge(a_kmm, done(e))
                    nc.scalar.copy(kT_all.rearrange("p (k n) -> p k n", k=NK)[:, :, ds(e.t * P, P)],
                                   bank[2 + u][:, 0:C].rearrange("p (k n) -> p k n", k=NK)).then_inc(a_kc, 1)
                    act.wait_ge(a_vmm, done(e))
                    nc.scalar.copy(v_all[:, ds(e.t * C, C)], bank[4 + u][:, 0:C]).then_inc(a_vc, 1)
                if e := back(s, 0):
                    nc.scalar.copy(xnT_all.rearrange("p (k n) -> p k n", k=NK)[:, :, ds(e.t * P, P)],
                                   bank[e.u][:, 0:C].rearrange("p (k n) -> p k n", k=NK)).then_inc(a_all, 1)
                if e := back(s, 3):
                    u = e.u
                    act.wait_ge(a_row, done(e))
                    act.dma_start(xt_t[e.t, :, :], xt_sb[:, u, :]).then_inc(a_tab[u], 16)
                    act.dma_start(al_t[e.t, :, :], xt_sb[:, u, C:C + HG]).then_inc(a_tab[u], 16)
                    act.wait_ge(a_hg, done(e))
                    nc.scalar.activation(hg_all[:, ds(e.t * GH, GH)], hgpre[:, u, :], ACT.Gelu).then_inc(a_gelu, 1)

            sweep(act, 3, step_a)
            act.wait_ge(s_kmax, 3)

            def step_k(s):
                act.wait_ge(k_tr, freed(s))
                for f in range(NK):
                    last = nc.scalar.activation(ek[:, s.u, f * P:(f + 1) * P], tile_of(kT_all, f, s), ACT.Exp,
                                                bias=nkmax[:, f:f + 1], accum_out=ksum[:, ds(s.t + f * NT, 1)])
                last.then_inc(k_exp, 1)

            sweep(act, 0, step_k)
            act.wait_ge(s_m1, 1)
            nc.scalar.copy(m1[:, :, :].rearrange("p k c -> p (k c)"), bank[4][:, 0:NK * C]).then_inc(s_m1c, 1)

            act.wait_ge(a_gelu, NT + 2)
            act.wait_ge(s_half, 2)

            def step_b(s):
                if e := back(s, 8):
                    act.wait_ge(b_lmm, done(e))
                    nc.scalar.copy(logits[:, ds(e.t * NE, NE)], bank[6 + e.u][:, C:C + NE]).then_inc(b_lc, 1)
                if e := back(s, 2):
                    act.wait_ge(b_alpha, done(e))
                    act.wait_ge(b_gn, freed(e))
                    nc.scalar.activation(sm[:, e.u, :], lg[:, e.u, HG:2 * HG], ACT.Exp, bias=lg[:, e.u, 2 * HG:2 * HG + 1],
                                         accum_out=lg[:, e.u, 2 * HG + 1:2 * HG + 2]).then_inc(b_exp, 1)
                if e := back(s, 0):
                    act.wait_ge(b_htr, freed(e))
                    nc.scalar.copy(hgb[:, e.u, :], hg_all[:, ds(e.t * GH, GH)]).then_inc(b_hgb, 1)
                if e := back(s, 2):
                    act.wait_ge(b_exp, done(e))
                    act.wait_ge(b_x2, freed(e))
                    nc.scalar.activation(tmp[:, e.u, :], xt_sb[:, e.u, 0:DG], ACT.Copy, scale=sm[:, e.u, 0:1]).then_inc(b_g0, 1)
                if e := back(s, 2):
                    act.wait_ge(b_gmm, done(e))
                    act.wait_ge(b_og, freed(e))
                    for f in range(NK):
                        last = nc.scalar.activation(sg[:, e.u, f * P:(f + 1) * P], bank[2 + e.u][:, P * (f + 1):P * (f + 2)],
                                                    ACT.Tanh, bias=vec[:, 2, f:f + 1], scale=0.5)
                    last.then_inc(b_sg, 1)
                if e := back(s, 1):
                    act.wait_ge(b_htr, done(e))
                    act.wait_ge(b_gmm, freed(e))
                    nc.scalar.copy(hgT[0:GH, e.u, :], bank[2 + e.u][0:GH, 0:P]).then_inc(b_hgT, 1)
                if e := back(s, 6):
                    act.wait_ge(b_x3, done(e))
                    act.wait_ge(b_r2, done(e))
                    act.wait_ge(b_x4o[e.u], left(e))
                    nc.scalar.activation(x4[:, e.u, :], xn[:, e.u, :], ACT.Copy, scale=r2[:, e.u, :]).then_inc(b_x4, 1)
                    act.wait_ge(b_tr, done(e))
                    act.wait_ge(b_lmm, freed(e))
                    nc.scalar.copy(xnT[:, e.u, :], bank[6 + e.u][:, 0:C]).then_inc(b_xnT, 1)

            sweep(act, 8, step_b)

            act.wait_ge(s_diff, 1)
            nc.scalar.activation(tok[:, 4, :], tok[:, 3, :], ACT.Exp).then_inc(s_exp, 1)

            act.wait_ge(s_low, 1)

            def weights(s, b, k, t):
                act.wait_ge(t_mm, s + 1)
                nc.scalar.activation(far[:, b, :], cols[:, 0:FT], ACT.Abs, scale=-1.0,
                                     bias=tok[:, 12 + 2 * k, ds(t, 1)]).then_inc(t_far, 1)
                act.wait_ge(t_far, s + 5)
                nc.scalar.activation(rv[:, b, FT:2 * FT], far[:, b, :], ACT.Relu, scale=tok[:, 9 + k, ds(t, 1)],
                                     bias=tok[:, 5 + k, ds(t, 1)]).then_inc(t_w, 1)

            with act.Fori(0, NT // 2) as i:
                for b in range(4):
                    weights(4 * i + b, b, b % 2, 2 * i + b // 2)
            act.wait_ge(s_slots, 1)

            def rowsT(t):
                act.wait_ge(f_x, t + 2)
                act.wait_ge(f_h[1], t + 1)
                e = act.value_load(te[0:1, ds(t, 1)], min_val=0, max_val=NE - 1)
                for k in range(NK):
                    last = nc.scalar.activation(xsT[:, k * P:(k + 1) * P], bank[0][:, k * P:(k + 1) * P], ACT.Identity,
                                                scale=flng_sb[:, ds(e + k * NE, 1)], bias=flnb_sb[:, ds(e + k * NE, 1)])
                last.then_inc(f_xc, 1)

            def gelu(t, j):
                act.wait_ge(f_hb[j], t + 2)
                act.wait_ge(f_t[j], t + 1)
                nc.scalar.activation(hid[:, j * HJ:(j + 1) * HJ], hpre[:, j * HJ:(j + 1) * HJ], ACT.Gelu
                                     ).then_inc(f_ge[j], 1)

            def hiddenT(t):
                act.wait_ge(f_t[1], t + 2)
                act.wait_ge(f_y[1], t + 1)
                nc.scalar.copy(hidT[:, HJ:2 * HJ], bank[7][:, :]).then_inc(f_tc[1], 1)

            rowsT(0)
            gelu(0, 0)
            gelu(0, 1)
            rowsT(1)
            with act.Fori(1, FT - 1) as t:
                hiddenT(t - 1)
                gelu(t, 0)
                gelu(t, 1)
                rowsT(t + 1)
            hiddenT(FT - 2)
            gelu(FT - 1, 0)
            gelu(FT - 1, 1)
            hiddenT(FT - 1)

        @block.vector
        def _(dve):
            chained = [0]

            def link(ins):
                chained[0] += 1
                ins.then_inc(s_r, 1)
                dve.wait_ge(s_r, chained[0])

            dve.wait_ge(s_w, 16 * 16)
            dve.wait_ge(s_pool, 12)
            nc.vector.tensor_scalar(vec[:, 2, :], vec[:, 2, :], 0.5, None, ALU.mult).then_inc(s_half, 1)
            nc.vector.tensor_scalar(wproj_sb[:, :, :], wproj_sb[:, :, :], 0.5, None, ALU.mult).then_inc(s_half, 1)
            for k in range(NK):
                for s in range(2):
                    link(nc.vector.tensor_tensor(sg[:, 0, :], wm[:, k, C:2 * C], attn_sb[:, s, :], ALU.mult))
                    link(nc.vector.tensor_reduce(wm[:, k, 2 * C + s * HG:2 * C + (s + 1) * HG],
                                                 sg[:, 0, :].rearrange("p (h d) -> p h d", h=HG), AX.X, ALU.add))
            for k in range(NK):
                nc.vector.tensor_copy(R3[:, 512 + k * P:512 + (k + 1) * P],
                                      vec[:, 1, k:k + 1].to_broadcast([P, P])).then_inc(s_lnb, 1)
            dve.wait_ge(s_bg, 1)
            nc.vector.tensor_tensor(bg1_sb[:, :], bg1_sb[:, :], bank[0][:, 0:GH], ALU.add).then_inc(s_prep, 1)
            for k in range(NK):
                nc.vector.tensor_scalar(wm[:, k, C + ROW:WM], wm[:, k, C + ROW:WM], vec[:, 0, k:k + 1], None,
                                        ALU.mult).then_inc(s_prep, 1)
            dve.wait_ge(s_prep, 1 + NK)

            def variances(s, mv_sem, s_out):
                u = s.u
                dve.wait_ge(mv_sem, done(s))
                nc.vector.tensor_scalar(va[:, u, 0:2], mv[:, u, 1:2].to_broadcast([P, 2]), EPS, None, ALU.add)
                nc.vector.tensor_scalar(va[:, u, 2:3], mv[:, u, 1:2], 1.0 + EPS, EPS * EPS, ALU.mult, ALU.add
                                        ).then_inc(s_out, 1)

            def stats_a(s):
                u = s.u
                dve.wait_ge(a_in[u], landed(s))
                nc.vector.bn_stats(st[:, u, :], x_sb[:, u, :]).then_inc(a_stats, 1)
                dve.wait_ge(a_stats, done(s))
                dve.wait_ge(a_pow, freed(s))
                dve.sem_inc(s_held[0], 1)
                nc.vector.bn_aggr(mv[:, u, :], st[:, u, :]).then_inc(a_mv, 1)
                variances(s, a_mv, a_va)

            def norm_a(s):
                u = s.u
                dve.wait_ge(a_pow, done(s))
                dve.wait_ge(a_tr, freed(s))
                nc.vector.tensor_scalar(xn[:, u, :], x_sb[:, u, :], mv[:, u, 0:1], rs[:, u, 0:1],
                                        ALU.subtract, ALU.mult).then_inc(a_xn, 1)

            def take_a(s):
                u = s.u
                dve.wait_ge(a_kc, done(s))
                nc.vector.tensor_reduce(kmax[:, :, ds(s.t, 1)],
                                        kT_all.rearrange("p (k n) -> p k n", k=NK)[:, :, ds(s.t * P, P)], AX.X, ALU.max)
                dve.wait_ge(a_gmm, done(s))
                dve.wait_ge(a_tab[u], left(s, 32))
                nc.vector.tensor_copy(xt_sb[:, u, :], bank[6 + u][:, 0:ROW]).then_inc(a_row, 1)
                dve.wait_ge(a_gelu, freed(s))
                dve.wait_ge(a_r2, done(s))
                nc.vector.scalar_tensor_tensor(out=hgpre[:, u, :], in0=bank[6 + u][:, ROW:ROW + GH], scalar=r2[:, u, :],
                                               in1=bg1_sb[:, :], op0=ALU.mult, op1=ALU.add).then_inc(a_hg, 1)

            def step_a(s):
                if e := back(s, 1):
                    norm_a(e)
                if back(s, 0):
                    stats_a(s)
                if e := back(s, 3):
                    take_a(e)

            sweep(dve, 3, step_a)
            kv = kT_all.rearrange("p (k n) -> p k n", k=NK)
            dve.wait_ge(a_hg, NT + 2)
            nc.vector.tensor_reduce(kmax[:, :, LAST:LAST + 1], kv[:, :, LAST * P:N], AX.X, ALU.max).then_inc(s_kmax, 1)
            dve.wait_ge(s_kmax, 1)
            nc.vector.tensor_reduce(nkmax[:, :], kmax[:, :, 0:LAST + 1], AX.X, ALU.max, negate=True).then_inc(s_kmax, 1)
            nc.vector.memset(kv[:, :, N:NP], -1e30).then_inc(s_kmax, 1)

            def step_k(s):
                dve.wait_ge(k_tr, done(s))
                dve.wait_ge(k_mm, freed(s))
                nc.vector.tensor_copy(ekT[:, s.u, :], bank[s.u][:, 0:C]).then_inc(k_cp, 1)

            sweep(dve, 0, step_k)
            dve.wait_ge(k_exp, NT + 2)
            link(nc.vector.tensor_reduce(kinv[:, 0, :], ksum[:, :].rearrange("p (k n) -> p k n", k=NK), AX.X, ALU.add))
            link(nc.vector.reciprocal(kinv[:, 1, :], kinv[:, 0, :]))
            dve.wait_ge(s_csum, 1)
            for f in range(NK):
                for h in range(P // DM):
                    r = slice(h * DM, (h + 1) * DM)
                    ins = nc.vector.tensor_scalar(ctx_bd[r, f, r], bank[2 + f][r, r], kinv[r, 1, f:f + 1], None, ALU.mult)
            ins.then_inc(s_ctx, 1)

            def mix_b(e):
                dve.wait_ge(b_pmm, done(e))
                dve.wait_ge(b_in[e.u], landed(e))
                nc.vector.tensor_tensor(x_sb[:, e.u, :], bank[4 + e.u][:, 0:C], x_sb[:, e.u, :], ALU.add).then_inc(b_mix, 1)

            def x2_b(e):
                dve.wait_ge(b_mix, done(e))
                dve.wait_ge(b_x2o[e.u], left(e))
                dve.wait_ge(b_gn, done(e))
                nc.vector.scalar_tensor_tensor(out=x2[:, e.u, :].rearrange("p (h d) -> p h d", h=HG),
                                               in0=tmp[:, e.u, :].unsqueeze(1).to_broadcast([P, HG, DG]),
                                               scalar=lg[:, e.u, 10:11],
                                               in1=x_sb[:, e.u, :].rearrange("p (h d) -> p h d", h=HG),
                                               op0=ALU.mult, op1=ALU.add).then_inc(b_x2, 1)

            def stats_b(e):
                dve.wait_ge(b_x2, done(e))
                nc.vector.bn_stats(st[:, e.u, :], x2[:, e.u, :]).then_inc(b_stats, 1)

            def aggr_b(e):
                dve.wait_ge(b_stats, done(e))
                dve.wait_ge(b_rstd, freed(e))
                dve.sem_inc(s_held[0], 1)
                nc.vector.bn_aggr(mv[:, e.u, :], st[:, e.u, :]).then_inc(b_mv, 1)

            def alpha_b(e):
                dve.wait_ge(b_gat[e.u], e.i * 32 + 32)
                dve.wait_ge(b_exp, freed(e))
                nc.vector.tensor_tensor(lg[:, e.u, 0:HG], g2[:, e.u, :], xt_sb[:, e.u, C + HG:ROW], ALU.add).then_inc(b_al, 1)

            def leaky_b(e):
                dve.wait_ge(b_al, done(e))
                nc.vector.scalar_tensor_tensor(out=lg[:, e.u, HG:2 * HG], in0=lg[:, e.u, 0:HG], scalar=0.01,
                                               in1=lg[:, e.u, 0:HG], op0=ALU.mult, op1=ALU.max).then_inc(b_lk, 1)

            def most_b(e):
                dve.wait_ge(b_lk, done(e))
                nc.vector.tensor_reduce(lg[:, e.u, 8:9], lg[:, e.u, HG:2 * HG], AX.X, ALU.max, negate=True
                                        ).then_inc(b_alpha, 1)

            def gate_b(e):
                dve.wait_ge(b_omm, done(e))
                dve.wait_ge(b_sg, done(e))
                dve.wait_ge(b_pmm, freed(e))
                nc.vector.scalar_tensor_tensor(out=og[:, e.u, :], in0=sg[:, e.u, :], scalar=1.0, in1=bank[e.u][:, 0:C],
                                               op0=ALU.add, op1=ALU.mult).then_inc(b_og, 1)

            def head_b(e, h, before, after):
                dve.wait_ge(before, done(e))
                if h == 1:
                    nc.vector.reciprocal(lg[:, e.u, 10:11], lg[:, e.u, 9:10])
                nc.vector.scalar_tensor_tensor(out=tmp[:, e.u, :], in0=xt_sb[:, e.u, h * DG:(h + 1) * DG],
                                               scalar=sm[:, e.u, h:h + 1], in1=tmp[:, e.u, :],
                                               op0=ALU.mult, op1=ALU.add).then_inc(after, 1)

            def norm_b(e):
                u = e.u
                dve.wait_ge(b_rstd, done(e))
                dve.wait_ge(b_tr, freed(e))
                dve.wait_ge(b_x4, freed(e))
                nc.vector.tensor_scalar(xn[:, u, :], x2[:, u, :], mv[:, u, 0:1], rs[:, u, 0:1],
                                        ALU.subtract, ALU.mult).then_inc(b_x3, 1)
                nc.vector.tensor_tensor(r2[:, u, :], rs[:, u, 1:2], rs[:, u, 2:3], ALU.mult).then_inc(b_r2, 1)

            def step_b(s):
                e1, e2, e3, e5 = (back(s, lag) for lag in (1, 2, 3, 5))
                if e5:
                    norm_b(e5)
                if e3:
                    mix_b(e3)
                if e2:
                    head_b(e2, 1, b_g0, b_g1)
                if e3:
                    x2_b(e3)
                if e2:
                    head_b(e2, 2, b_g1, b_g2)
                    gate_b(e2)
                    head_b(e2, 3, b_g2, b_gn)
                if e3:
                    stats_b(e3)
                if e1:
                    alpha_b(e1)
                if e3:
                    aggr_b(e3)
                if e1:
                    leaky_b(e1)
                if e3:
                    variances(e3, b_mv, b_va)
                if e1:
                    most_b(e1)

            sweep(dve, 5, step_b)

            dve.wait_ge(b_lc, NT + 2)
            dve.wait_ge(s_pool, 13)
            for u in range(2):
                dve.wait_ge(b_x2o[u], 16 * (NT // 2 + 1))
                dve.wait_ge(b_x4o[u], 16 * (NT // 2 + 1))
            te3 = lambda a: a.rearrange("p (t e) -> p t e", e=NE)
            wide = lambda a: a.unsqueeze(2).to_broadcast([P, NT, NE])
            desc3 = desc[:, :].unsqueeze(1).to_broadcast([P, NT, NE])
            TOK, M, D, DIFF, EXP, W, SLOT = 0, 1, 2, 3, 4, 5, 7
            link(nc.vector.tensor_tensor(te3(logits), te3(logits), br_sb[:, :].unsqueeze(1).to_broadcast([P, NT, NE]), ALU.add))
            for k in range(2):
                of = work if k else logits
                m, d = tok[:, 9 + k, :], tok[:, D, :]
                link(nc.vector.tensor_reduce(m, te3(of), AX.X, ALU.max))
                link(nc.vector.tensor_tensor(te3(chosen), te3(of), wide(m), ALU.is_equal))
                link(nc.vector.tensor_tensor(te3(chosen), te3(chosen), desc3, ALU.mult))
                link(nc.vector.tensor_reduce(d, te3(chosen), AX.X, ALU.max))
                link(nc.vector.tensor_tensor(te3(oh[k]), desc3, wide(d), ALU.is_equal))
                if k == 0:
                    link(nc.vector.scalar_tensor_tensor(out=work, in0=oh[0], scalar=-BIG, in1=logits,
                                                        op0=ALU.mult, op1=ALU.add))
            link(nc.vector.tensor_scalar(tok[:, M, :], tok[:, TOK, :], float(N), None, ALU.is_lt))
            link(nc.vector.tensor_tensor(chosen, oh[0], oh[1], ALU.add))
            link(nc.vector.tensor_tensor(te3(chosen), te3(chosen), wide(tok[:, M, :]), ALU.mult))
            nc.vector.tensor_tensor(tok[:, DIFF, :], tok[:, 10, :], tok[:, 9, :], ALU.subtract).then_inc(s_diff, 1)
            dve.sem_inc(s_chosen, 1)
            dve.wait_ge(s_exp, 1)
            link(nc.vector.tensor_scalar(tok[:, D, :], tok[:, EXP, :], 1.0, None, ALU.add))
            link(nc.vector.reciprocal(tok[:, W, :], tok[:, D, :]))
            link(nc.vector.tensor_tensor(tok[:, W + 1, :], tok[:, EXP, :], tok[:, W, :], ALU.mult))
            link(nc.vector.tensor_scalar(tok[:, 9:11, :], tok[:, W:W + 2, :], -1.0, None, ALU.mult))
            dve.wait_ge(s_tot, 1)
            nc.vector.tensor_copy(ttb[0:NT, :].rearrange("p (e c) -> p e c", e=NE),
                                  bank[0][0:NT, 0:NE].unsqueeze(2).to_broadcast([NT, NE, P])).then_inc(s_ttb, 1)
            dve.wait_ge(s_pos, 1)
            link(nc.vector.tensor_copy(pos, bank[1][:, 0:NE * (NT + 1)]))
            pos3 = pos.rearrange("p (e t) -> p e t", e=NE)
            nc_e, size, base, end = (small[:, j, :] for j in range(4))
            link(nc.vector.tensor_scalar(small_i[:, 0, :], pos3[:, :, NT], float(P - 1), None, ALU.add))
            link(nc.vector.tensor_scalar(small_i[:, 1, :], small_i[:, 0, :], -P, None, ALU.bitwise_and))
            link(nc.vector.tensor_copy(size, small_i[:, 1, :]))
            link(nc.vector.memset(base[:, 0:1], 0.0))
            for e in range(NE):
                link(nc.vector.tensor_tensor(end[:, e:e + 1], base[:, e:e + 1], size[:, e:e + 1], ALU.add))
                if e + 1 < NE:
                    link(nc.vector.tensor_copy(base[:, e + 1:e + 2], end[:, e:e + 1]))
            link(nc.vector.tensor_scalar(sl[:, 0, :], cols[:, 0:FT], float(P), None, ALU.mult))
            link(nc.vector.tensor_scalar(sl[:, 1, :], sl[:, 0, :], end[:, 0:1], None, ALU.is_ge))
            for e in range(1, NE - 1):
                link(nc.vector.scalar_tensor_tensor(out=sl[:, 1, :], in0=sl[:, 0, :], scalar=end[:, e:e + 1],
                                                    in1=sl[:, 1, :], op0=ALU.is_ge, op1=ALU.add))
            link(nc.vector.tensor_copy(te, sl[0:1, 1, :]))
            pos_te = pos3[:, :, 0:NT]
            link(nc.vector.tensor_tensor(pos_te, pos_te, base.unsqueeze(2).to_broadcast([P, NE, NT]), ALU.add))
            link(nc.vector.tensor_scalar(tok[:, D, :], tok[:, M, :], -1000.0, 1000.0, ALU.mult, ALU.add))
            for k in range(2):
                slot = tok[:, SLOT + k, :]
                link(nc.vector.tensor_tensor(te3(work), te3(oh[k]), pos_te.rearrange("p e t -> p t e"), ALU.mult))
                link(nc.vector.tensor_reduce(slot, te3(work), AX.X, ALU.add))
                si, lo, hi = (tok_i[:, 3 * k + j, :] for j in range(3))
                link(nc.vector.tensor_copy(si, slot))
                link(nc.vector.tensor_scalar(lo, si, P - 1, None, ALU.bitwise_and))
                link(nc.vector.tensor_scalar(hi, si, 7, None, ALU.logical_shift_right))
                link(nc.vector.tensor_copy(tok[:, 11 + 2 * k, :], lo))
                link(nc.vector.tensor_tensor(tok[:, 11 + 2 * k, :], tok[:, 11 + 2 * k, :], tok[:, D, :], ALU.add))
                link(nc.vector.tensor_copy(tok[:, 12 + 2 * k, :], hi))
            link(nc.vector.tensor_scalar(tok[:, DIFF, :], tok[:, TOK, :], 1.0, None, ALU.add))

            dve.sem_inc(s_low, 1)

            def onehots(s, b, k, t):
                dve.wait_ge(t_mm, s + 1)
                nc.vector.tensor_scalar(ohb[:, b, :], cols[:, :], tok[:, 11 + 2 * k, ds(t, 1)], None,
                                        ALU.is_equal).then_inc(t_oh, 1)
                nc.vector.tensor_scalar(rv[:, b, 0:FT], cols[:, 0:FT], tok[:, 12 + 2 * k, ds(t, 1)],
                                        tok[:, DIFF, ds(t, 1)], ALU.is_equal, ALU.mult).then_inc(t_idx, 1)

            with dve.Fori(0, NT // 2) as i:
                for b in range(4):
                    onehots(4 * i + b, b, b % 2, 2 * i + b // 2)
            dve.wait_ge(s_table, 1)
            link(nc.vector.tensor_scalar(sl[:, 0, :], bank[2][:, 0:FT], 1.0, None, ALU.subtract))
            link(nc.vector.tensor_copy(slot_w, bank[2][:, FT:2 * FT]))
            link(nc.vector.tensor_scalar(gidx, sl[:, 0, :], 0.0, None, ALU.max))
            link(nc.vector.tensor_scalar(sl[:, 1, :], sl[:, 0, :], 0.0, None, ALU.is_lt))
            nc.vector.scalar_tensor_tensor(out=sidx, in0=sl[:, 1, :], scalar=dummy[:, 0:1], in1=sl[:, 0, :],
                                           op0=ALU.mult, op1=ALU.add).then_inc(s_slots, 1)

            dve.wait_ge(s_b1, 16)
            dve.wait_ge(s_b2, 16)

            def bias(t, e):
                for j in range(2):
                    dve.wait_ge(f_h[j], t + 2)
                    dve.wait_ge(f_ge[j], t + 1)
                    nc.vector.tensor_tensor(hpre[:, j * HJ:(j + 1) * HJ], bank[4 + j][:, :],
                                            b1_all[:, ds(e * HID + j * HJ, HJ)], ALU.add).then_inc(f_hb[j], 1)

            def hiddenT(t):
                dve.wait_ge(f_t[0], t + 2)
                dve.wait_ge(f_y[0], t + 1)
                nc.vector.tensor_copy(hidT[:, 0:HJ], bank[6][:, :]).then_inc(f_tc[0], 1)

            def rows(t, e):
                dve.wait_ge(f_y[1], t + 2)
                dve.wait_ge(f_yw, t + 1)
                nc.vector.tensor_tensor(y1, bank[1][:, 0:C], b2_all[:, ds(e * C, C)], ALU.add).then_inc(f_y1, 1)
                dve.wait_ge(f_y1, t + 2)
                if not (isinstance(t, int) and t == 0):
                    dve.wait_ge(f_add, 16 * t)
                nc.vector.tensor_scalar(yw, y1, slot_w[:, ds(t, 1)], None, ALU.mult).then_inc(f_yw, 1)

            def expert(t):
                return dve.value_load(te[0:1, ds(t, 1)], min_val=0, max_val=NE - 1)

            bias(0, expert(0))
            hiddenT(0)
            bias(1, expert(1))
            hiddenT(1)
            rows(0, expert(0))
            with dve.Fori(2, FT) as t:
                bias(t, expert(t))
                hiddenT(t)
                rows(t - 1, expert(t - 1))
            rows(FT - 1, expert(FT - 1))

        @block.tensor
        def _(pe):
            pe.wait_ge(s_lnb, NK)
            for k in range(NK):
                mm = nc.tensor.matmul(bank[0][:, 0:GH], R3[:, 512 + k * P:512 + (k + 1) * P], wm[:, k, C + ROW:WM],
                                      start=(k == 0), stop=(k == NK - 1))
            mm.then_inc(s_bg, 1)
            pe.wait_ge(s_prep, 1 + NK)

            def turn(out, src, s_out):
                for k in range(NK):
                    mm = nc.tensor.transpose(out[:, k * P:(k + 1) * P], src[:, k * P:(k + 1) * P], ident[:, :])
                mm.then_inc(s_out, 1)

            def project_a(s):
                u = s.u
                pe.wait_ge(a_xnT, done(s))
                pe.wait_ge(a_kc, freed(s))
                for f in range(NK):
                    for k in range(NK):
                        mm = nc.tensor.matmul(bank[2 + u][:, f * P:(f + 1) * P], wk_sb[:, k, f * P:(f + 1) * P],
                                              xnT[:, u, k * P:(k + 1) * P], start=(k == 0), stop=(k == NK - 1))
                mm.then_inc(a_kmm, 1)
                pe.wait_ge(a_vc, freed(s))
                for k in range(NK):
                    mm = nc.tensor.matmul(bank[4 + u][:, 0:C], xnT[:, u, k * P:(k + 1) * P], wm[:, k, 0:C],
                                          start=(k == 0), stop=(k == NK - 1))
                mm.then_inc(a_vmm, 1)
                pe.wait_ge(a_hg, freed(s))
                for k in range(NK):
                    mm = nc.tensor.matmul(bank[6 + u][:, 0:ROW + GH], xnT[:, u, k * P:(k + 1) * P], wm[:, k, C:WM],
                                          start=(k == 0), stop=(k == NK - 1))
                mm.then_inc(a_gmm, 1)

            def step_a(s):
                if e := back(s, 0):
                    pe.wait_ge(a_xn, done(e))
                    pe.wait_ge(a_all, freed(e))
                    turn(bank[e.u], xn[:, e.u, :], a_tr)
                if e := back(s, 1):
                    project_a(e)

            sweep(pe, 1, step_a)

            def zeros(outs, **flags):
                for o in outs:
                    mm = nc.tensor.matmul(o, zrow[:, 0:P], zrow[:, 0:o.shape[1]], **flags)
                return mm

            def step_k(s):
                if e := back(s, 0):
                    pe.wait_ge(k_exp, done(e))
                    pe.wait_ge(k_cp, freed(e))
                    turn(bank[e.u], ek[:, e.u, :], k_tr)
                if e := back(s, 1):
                    pe.wait_ge(k_cp, done(e))
                    for f in range(NK):
                        mm = nc.tensor.matmul(bank[2 + f][:, 0:P], ekT[:, e.u, f * P:(f + 1) * P],
                                              v_all[:, ds(e.t * C + f * P, P)], start=False, stop=False)
                    mm.then_inc(k_mm, 1)

            pe.wait_ge(a_kc, NT + 2)
            sums = [bank[2][:, 0:P], bank[3][:, 0:P]]
            zeros(sums, start=True, stop=False)
            sweep(pe, 1, step_k)
            zeros(sums, start=False, stop=True).then_inc(s_csum, 1)
            pe.wait_ge(s_ctx, 1)
            for k in range(NK):
                for f in range(NK):
                    mm = nc.tensor.matmul(bank[4][:, k * C + f * P:k * C + (f + 1) * P], wqT_sb[:, f, k * P:(k + 1) * P],
                                          ctx_bd[:, f, :], start=True, stop=True)
            mm.then_inc(s_m1, 1)
            pe.wait_ge(s_m1c, 1)
            pe.wait_ge(s_half, 2)

            def step_b(s):
                if e := back(s, 3):
                    pe.wait_ge(b_og, done(e))
                    pe.wait_ge(b_mix, freed(e))
                    for f in range(NK):
                        mm = nc.tensor.matmul(bank[4 + e.u][:, 0:C], og[:, e.u, f * P:(f + 1) * P], wproj_sb[:, f, :],
                                              start=(f == 0), stop=(f == NK - 1))
                    mm.then_inc(b_pmm, 1)
                if e := back(s, 1):
                    pe.wait_ge(b_og, freed(e))
                    for f in range(NK):
                        for k in range(NK):
                            mm = nc.tensor.matmul(bank[e.u][:, f * P:(f + 1) * P], m1[:, k, f * P:(f + 1) * P],
                                                  tile_of(xnT_all, k, e), start=(k == 0), stop=(k == NK - 1))
                    mm.then_inc(b_omm, 1)
                if e := back(s, 6):
                    pe.wait_ge(b_x3, done(e))
                    pe.wait_ge(b_lc, freed(e))
                    turn(bank[6 + e.u], xn[:, e.u, :], b_tr)
                if e := back(s, 0):
                    pe.wait_ge(b_hgb, done(e))
                    pe.wait_ge(b_sg, freed(e))
                    pe.sem_inc(s_held[1], 1)
                    nc.tensor.transpose(bank[2 + e.u][0:GH, 0:P], hgb[:, e.u, :], ident[:, :]).then_inc(b_htr, 1)
                if e := back(s, 7):
                    pe.wait_ge(b_xnT, done(e))
                    for k in range(NK):
                        mm = nc.tensor.matmul(bank[6 + e.u][:, C:C + NE], xnT[:, e.u, k * P:(k + 1) * P], wr_sb[:, k, :],
                                              start=(k == 0), stop=(k == NK - 1))
                    mm.then_inc(b_lmm, 1)
                if e := back(s, 1):
                    pe.wait_ge(b_hgT, done(e))
                    for f in range(NK):
                        mm = nc.tensor.matmul(bank[2 + e.u][:, (f + 1) * P:(f + 2) * P], wg2_sb[:, f * P:(f + 1) * P],
                                              hgT[0:GH, e.u, :], start=True, stop=True)
                    mm.then_inc(b_gmm, 1)

            sweep(pe, 7, step_b)

            pe.wait_ge(s_chosen, 1)
            ch3 = chosen.rearrange("p (t e) -> p t e", e=NE)
            for e in range(NE):
                mm = nc.tensor.matmul(bank[0][0:NT, e:e + 1], ch3[:, :, e], ones[:, 0:1], start=True, stop=True)
            mm.then_inc(s_tot, 1)
            pe.wait_ge(s_ttb, 1)
            for e in range(NE):
                at = e * (NT + 1)
                nc.tensor.matmul(bank[1][:, at:at + NT + 1], ttb[0:NT, e * P:(e + 1) * P], upper[0:NT, 0:NT + 1],
                                 start=True, stop=False)
                mm = nc.tensor.matmul(bank[1][:, at:at + NT], upper[:, :], ch3[:, :, e], start=False, stop=True)
            mm.then_inc(s_pos, 1)
            table = bank[2][:, 0:2 * FT]
            zeros([table], start=True, stop=False)
            with pe.Fori(0, NT // 2) as i:
                for b in range(4):
                    s = 4 * i + b
                    pe.wait_ge(t_oh, s + 5)
                    pe.wait_ge(t_idx, s + 5)
                    pe.wait_ge(t_w, s + 5)
                    nc.tensor.matmul(table, ohb[:, b, :], rv[:, b, :], start=False, stop=False).then_inc(t_mm, 1)
            zeros([table], start=False, stop=True).then_inc(s_table, 1)

            def expert(t):
                return pe.value_load(te[0:1, ds(t, 1)], min_val=0, max_val=NE - 1)

            def rows(t):
                pe.wait_ge(f_gat, 16 * t + 16)
                pe.wait_ge(f_xc, t + 1)
                turn(bank[0], xs, f_x)

            def hidden(t, e, j):
                pe.wait_ge(f_xc, t + 2)
                pe.wait_ge(f_hb[j], t + 1)
                for k in range(NK):
                    mm = nc.tensor.matmul(bank[4 + j][:, :], xsT[:, k * P:(k + 1) * P],
                                          w1_all[:, ds(e * (NK * HID) + k * HID + j * HJ, HJ)],
                                          start=(k == 0), stop=(k == NK - 1))
                mm.then_inc(f_h[j], 1)

            def hidden_turn(t, j):
                pe.wait_ge(f_ge[j], t + 2)
                pe.wait_ge(f_tc[j], t + 1)
                for c in range(HC):
                    mm = nc.tensor.transpose(bank[6 + j][:, c * P:(c + 1) * P],
                                             hid[:, j * HJ + c * P:j * HJ + (c + 1) * P], ident[:, :])
                mm.then_inc(f_t[j], 1)

            def second(t, e, j):
                pe.wait_ge(f_tc[j], t + 2)
                if j == 0:
                    pe.wait_ge(f_y1, t + 1)
                for c in range(HC):
                    mm = nc.tensor.matmul(bank[1][:, 0:C], hidT[:, j * HJ + c * P:j * HJ + (c + 1) * P],
                                          w2_all[:, ds(e * (2 * HC * C) + (j * HC + c) * C, C)],
                                          start=(j == 0 and c == 0), stop=(j == 1 and c == HC - 1))
                mm.then_inc(f_y[j], 1)

            pe.wait_ge(s_w1, 16)
            pe.wait_ge(s_w2, 16)
            pe.wait_ge(s_slots, 1)
            rows(0)
            e = expert(0)
            hidden(0, e, 0)
            hidden(0, e, 1)
            rows(1)
            hidden_turn(0, 0)
            with pe.Fori(1, FT - 1) as t:
                now, last = expert(t), expert(t - 1)
                hidden(t, now, 0)
                hidden_turn(t - 1, 1)
                second(t - 1, last, 0)
                hidden(t, now, 1)
                rows(t + 1)
                hidden_turn(t, 0)
                second(t - 1, last, 1)
            now, last = expert(FT - 1), expert(FT - 2)
            hidden(FT - 1, now, 0)
            hidden_turn(FT - 2, 1)
            second(FT - 2, last, 0)
            hidden(FT - 1, now, 1)
            hidden_turn(FT - 1, 0)
            second(FT - 2, last, 1)
            hidden_turn(FT - 1, 1)
            second(FT - 1, now, 0)
            second(FT - 1, now, 1)


def kernel(x, src, dst, L0_gnn_weight, L0_gnn_attn_l, L0_gnn_attn_r, L0_mix_Wqkv, L0_mix_Wproj, L0_mix_bproj,
           L0_mix_ln_g, L0_mix_ln_b, L0_mix_Wg1, L0_mix_bg1, L0_mix_Wg2, L0_mix_bg2, L0_ffn_Wr, L0_ffn_br,
           L0_ffn_ln_g, L0_ffn_ln_b, L0_ffn_W1, L0_ffn_b1, L0_ffn_W2, L0_ffn_b2):
    import numpy as np
    import concourse.bacc as bacc
    from concourse.bass_utils import run_bass_kernel_spmd as run

    def chunks(w):
        w = np.asarray(w)
        return w.reshape(-1, P, w.shape[-1]).transpose(1, 0, 2)

    def rows(v):
        v = np.asarray(v).reshape(1, -1)
        return np.broadcast_to(v, (P, v.shape[1]))

    def columns(v):
        v = np.asarray(v)
        v = v.reshape(-1, NK, P).transpose(2, 1, 0)
        return v.reshape(P, -1)

    def tokens(a):
        padded = np.zeros(NP, np.asarray(a).dtype)
        padded[:N] = np.asarray(a)[:N]
        return padded.reshape(NT, P).T

    wqkv = np.asarray(L0_mix_Wqkv)
    xp = np.zeros((NP, C), np.float32)
    xp[:N] = np.asarray(x)
    attn = np.stack([np.asarray(L0_gnn_attn_l).reshape(-1), np.asarray(L0_gnn_attn_r).reshape(-1)])
    w1 = np.asarray(L0_ffn_W1).reshape(NE, NK, P, HID).transpose(2, 0, 1, 3).reshape(P, -1)
    w2 = np.asarray(L0_ffn_W2).reshape(NE, HID // P, P, C).transpose(2, 0, 1, 3).reshape(P, -1)
    vecs = np.stack([columns(v) for v in (L0_mix_ln_g, L0_mix_ln_b, L0_mix_bg2)], axis=1)
    arrays = {
        "x": xp, "edges": np.stack([tokens(dst), tokens(src)], axis=2).reshape(P, -1),
        "wk": chunks(wqkv[:, C:2 * C]), "wqT": chunks(wqkv[:, 0:C].T), "wv": chunks(wqkv[:, 2 * C:3 * C]),
        "wgnn": chunks(L0_gnn_weight), "attn": np.broadcast_to(attn[None], (P, 2, C)),
        "wproj": chunks(L0_mix_Wproj), "bproj": rows(L0_mix_bproj), "vecs": vecs,
        "wg1": chunks(L0_mix_Wg1), "bg1": rows(L0_mix_bg1), "wg2": np.asarray(L0_mix_Wg2),
        "wr": chunks(L0_ffn_Wr), "br": rows(L0_ffn_br), "flng": columns(L0_ffn_ln_g), "flnb": columns(L0_ffn_ln_b),
        "w1": w1, "b1": np.asarray(L0_ffn_b1).reshape(1, -1), "w2": w2, "b2": rows(L0_ffn_b2),
    }
    arrays = {k: np.ascontiguousarray(a) for k, a in arrays.items()}
    nc = bacc.Bacc("TRN2", target_bir_lowering=False, num_devices=1)
    args = {k: nc.dram_tensor(k + "_in", a.shape, mybir.dt.from_np(a.dtype), kind="ExternalInput").ap()
            for k, a in arrays.items()}
    fp32 = mybir.dt.float32
    args["out"] = nc.dram_tensor("rows_out", (NP + P, C), fp32, kind="ExternalOutput").ap()
    for name, shape in (("xt_table", (NP, ROW)), ("al_table", (NP, HG)), ("x4_table", (NP, C)),
                        ("xb_table", (NP, C))):
        args[name] = nc.dram_tensor(name, shape, fp32, kind="Internal").ap()
    gps_layer(nc, **args)
    r = run(nc, [{k + "_in": a for k, a in arrays.items()}], core_ids=[0])
    return np.asarray(r.results[0]["rows_out"])[:N]
```

```python
import concourse.bass as bass
from concourse import mybir
from contextlib import ExitStack
from collections import namedtuple

P = 128
N, C = 6250, 256
NT = 50
NP = NT * P
LAST = N // P
NK = C // P
HG, DG = 4, 64
DM = 32
GH = C // 4
NE, HID = 8, 1024
HJ = HID // 2
HC = HJ // P
FT = (2 * N + NE * (P - 1)) // P
ROW = C + 2 * HG
KV = 2 * C + 2
WM = 2 * C + ROW + GH
TURN = 10
EPS = 1e-5
BIG = 3.0e38

Tile = namedtuple("Tile", "t u i w q")


def back(tile, lag, count=NT):
    t, u, w = tile.t - lag, (tile.u - lag) % 2, (tile.w - lag) % 4
    if isinstance(t, int) and not 0 <= t < count:
        return None
    return Tile(t, u, tile.i + (tile.u - lag - u) // 2, w, tile.q + (tile.w - lag - w) // 4)


def sweep(eng, last_lag, step, count=NT, by=2):
    lead = by * max(1, (last_lag + by - 1) // by)
    for s in range(lead):
        step(Tile(s, s % 2, s // 2, s % 4, s // 4))
    with eng.Fori(lead // by, count // by) as n:
        for j in range(by):
            step(Tile(by * n + j, j % 2, by // 2 * n + j // 2, j % 4, by // 4 * n + j // 4))
    for s in range(count - count % by, count + last_lag):
        step(Tile(s, s % 2, s // 2, s % 4, s // 4))


def done(tile):
    return tile.t + 3


def freed(tile):
    return tile.t + 1


def landed(tile, each=16):
    return tile.i * each + 2 * each


def left(tile, each=16):
    return tile.i * each + each


def gps_layer(nc, x, edges, wk, wqT, wv, wgnn, attn, wproj, bproj, vecs, wg1, bg1, wg2,
              wr, br, flng, flnb, w1, b1, w2, b2, out, xt_table, al_table, x4_table, xb_table):
    fp32, i32 = mybir.dt.float32, mybir.dt.int32
    ALU = mybir.AluOpType
    ACT = mybir.ActivationFunctionType
    AX = mybir.AxisListType
    ds = bass.ds

    with ExitStack() as ctx:
        def sb(name, shape, dt=fp32):
            return ctx.enter_context(nc.sbuf_tensor(name, shape, dt))

        R1 = sb("R1", [P, NT * KV])
        kv_all = R1[:, :]
        w1_all = R1[:, 0:NE * NK * HID]
        w1_tile = R1[:, NE * NK * HID:(NE + 2) * NK * HID].rearrange("p (u c) -> p u c", u=2)
        R2 = sb("R2", [P, NE * NK * HID])
        xnT_all, hg_all = R2[:, 0:NK * NP], R2[:, NK * NP:NK * NP + NT * GH]
        w2_all = R2
        RA = sb("RA", [P, NK * WM + 2 * C])
        wm = RA[:, 0:NK * WM].rearrange("p (k c) -> p k c", k=NK)
        attn_sb = RA[:, NK * WM:NK * WM + 2 * C].rearrange("p (s c) -> p s c", s=2)
        b2_all = RA[:, 0:NE * C]
        R3 = sb("R3", [P, 5120])

        def pair(at, width):
            return R3[:, at:at + 2 * width].rearrange("p (u c) -> p u c", u=2)

        x_sb, xn, xnT, xt_sb = pair(0, C), pair(512, C), pair(1024, C), pair(1536, ROW)
        sg, og, x2, x4 = pair(2064, C), pair(2576, C), pair(3088, C), pair(3600, C)
        tmp, hgT, hgb, hgpre = pair(4112, DG), pair(4240, P), pair(4496, GH), pair(4624, GH)
        kd, ek = pair(3600, 2 * C), pair(2064, 2 * C)
        k_most, k_row, k_wide = R3[:, 4752:4752 + C], R3[:, 1024:1024 + C], R3[:, 1280:1280 + C]
        ttb = R3[:, 1024:1024 + NE * P]
        rv, ohb, far = (R3[:, a:a + 4 * w].rearrange("p (b c) -> p b c", b=4) for a, w in ((0, 2 * FT), (1050, P), (1562, FT)))
        xs = R3[:, 0:C]
        hidT = R3[:, 512:512 + 2 * HID].rearrange("p (u c) -> p u c", u=2)
        xsT, yw, y1 = pair(2560, C), pair(3072, C), R3[:, 3584:3584 + C]
        wqT_sb = sb("wqT_sb", [P, NK, C])
        R4 = sb("R4", [P, 2 * NK * C])
        wproj_sb, m1 = (R4[:, j * NK * C:(j + 1) * NK * C].rearrange("p (k c) -> p k c", k=NK) for j in range(2))
        wg2_sb = sb("wg2_sb", [GH, C])
        bproj_sb, bg1_sb, br_sb = sb("bproj_sb", [P, C]), sb("bg1_sb", [P, GH]), sb("br_sb", [P, NE])
        vec = sb("vec", [P, 3, NK])
        wr_sb = sb("wr_sb", [P, NK, NE])
        flng_sb, flnb_sb = sb("flng_sb", [P, NK * NE]), sb("flnb_sb", [P, NK * NE])
        b1_sb = sb("b1_sb", [P, NE * 2 * HC])
        ident, ones, upper = sb("ident", [P, P]), sb("ones", [P, P]), sb("upper", [P, P])
        cols = sb("cols", [P, P])
        ctx_bd = sb("ctx_bd", [P, NK, P])
        edges_i = sb("edges_i", [P, NT * 2], i32)
        idx = sb("idx", [P, 8], i32)
        st, mv = sb("st", [P, 2, 6]), sb("mv", [P, 2, 2])
        va, rs, r2 = (sb(n, [P, 2, w]) for n, w in (("va", 3), ("rs", 3), ("r2", 1)))
        cexp = sb("cexp", [P, 3])
        k_col, kinv = sb("k_col", [P, NK]), sb("kinv", [P, NK])
        xt_rows = R1[:, 0:4 * ROW].rearrange("p (w c) -> p w c", w=4)
        g2, lg, sm = sb("g2", [P, 4, HG]), sb("lg", [P, 2, 3 * HG]), sb("sm", [P, 2, 4])
        TE = NT * NE
        logits = wqT_sb[:, :, :].rearrange("p k c -> p (k c)")[:, 0:TE]
        work, chosen, oh0, oh1 = (R3[:, 2048 + j * TE:2048 + (j + 1) * TE] for j in range(4))
        oh = [oh0, oh1]
        pos = R3[:, 2048 + 4 * TE:2048 + 5 * TE + NE]
        tok = R4[:, 0:16 * NT].rearrange("p (j t) -> p j t", t=NT)
        tok_i = R3[:, 4352:4352 + 6 * NT].bitcast(i32).rearrange("p (j t) -> p j t", t=NT)
        gidx, sidx, slot_w, te = (R3[:, 4652 + j * FT:4652 + (j + 1) * FT] for j in range(4))
        gidx, sidx, te = gidx.bitcast(i32), sidx.bitcast(i32), te[0:1, :].bitcast(i32)
        sl = R3[:, 840:840 + 2 * FT].rearrange("p (j t) -> p j t", j=2)
        desc = sb("desc", [P, NE])
        small, bounds = sb("small", [P, NE]), sb("bounds", [P, NE + 1])
        small_i = sb("small_i", [P, 2, NE], i32)
        dummy = sb("dummy_row", [P, 1])
        zrow = sb("zrow", [P, C])
        bank = [ctx.enter_context(nc.psum_tensor(f"bank{b}", [P, 512], fp32)) for b in range(8)]

        at_start = {}

        def counts(prefix, names, start):
            made = [ctx.enter_context(nc.semaphore(f"{prefix}_{n}")) for n in names.split()]
            for s in made:
                at_start[id(s)] = (s, start)
            return made

        a_stats, a_mv, a_va, a_pow, a_r2, a_xn, a_tr, a_xnT, a_all, a_xb = counts(
            "a", "stats mv va pow r2 xn tr xnT all xb", 2)
        a_kvmm, a_gmm, a_kvc, a_most, a_row, a_hg, a_gelu = counts(
            "a", "kvmm gmm kvc most row hg gelu", 2)
        k_sub, k_exp, k_mm = counts("k", "sub exp mm", 2)
        b_omm, b_htr, b_hgT, b_gmm, b_sg, b_og, b_pmm = counts("b", "omm htr hgT gmm sg og pmm", 2)
        b_hgb, b_idx, b_al, b_lk, b_alpha, b_exp = counts("b", "hgb idx al lk alpha exp", 2)
        b_g0, b_g1, b_g2, b_gn, b_mix, b_x2, b_stats, b_mv = counts("b", "g0 g1 g2 gn mix x2 stats mv", 2)
        b_va, b_rstd, b_r2, b_x3, b_x4, b_tr, b_xnT, b_lmm, b_lc = counts(
            "b", "va rstd r2 x3 x4 tr xnT lmm lc", 2)
        t_oh, t_idx, t_mm = counts("t", "oh idx mm", 4)
        t_far, t_w = counts("t", "far0 far1 far2", 1), counts("t", "w0 w1 w2 w3", 1)
        f_gi, f_si, f_x, f_xe, f_h, f_ge, f_y, f_y1, f_yw = counts("f", "gi si x xe hmm gelu ymm y1 yw", 1)
        f_w1 = counts("f", "w1a w1b", 1)
        a_in, a_xbo, b_in = counts("a", "in0 in1", 16), counts("a", "xbo0 xbo1", 16), counts("b", "in0 in1", 16)
        a_tab = counts("a", "tab0 tab1", 32)
        b_x2o, b_x4o = counts("b", "x2o0 x2o1", 16), counts("b", "x4o0 x4o1", 16)
        b_gat, (f_gat, f_add) = counts("b", "gat0 gat1 gat2 gat3", 0), counts("f", "gat add", 0)
        (s_w, s_wb, s_pool, s_half, s_lnb, s_bg, s_prep, s_pad, s_most, s_col, s_wide, s_krow, s_csum, s_ctx, s_m1, s_m1c, s_w1, s_w2, s_b2,
         s_r, s_chosen, s_tot, s_ttb, s_pos, s_diff, s_exp, s_low, s_table, s_slots, s_dummy) = counts(
            "s", "w wb pool half lnb bg prep pad most col wide krow csum ctx m1 m1c w1 w2 b2 r chosen tot ttb pos diff exp low table slots dummy", 0)

        s_held = counts("s", "held_dve held_pe held_pool", 0)

        block = ctx.enter_context(nc.Block())
        x_t, out_t, xt_t, al_t, x4_t, xb_t = (a.rearrange("(t p) c -> t p c", p=P)
                                        for a in (x, out, xt_table, al_table, x4_table, xb_table))

        def tile_of(all_tokens, k, tile):
            return all_tokens[:, ds(tile.t * P + k * NP, P)]

        @block.sync
        def _(sp):
            for t, a in ((wm[:, :, 2 * C:3 * C], wgnn), (attn_sb, attn), (wm[:, :, 2 * C + ROW:WM], wg1), (vec, vecs),
                         (bg1_sb, bg1), (wm[:, :, 0:C], wk), (wm[:, :, C:2 * C], wv), (bproj_sb, bproj)):
                sp.dma_start(t if isinstance(t, bass.AP) else t[:], a).then_inc(s_w, 16)

            def load_a(s):
                sp.lower_val(s.t), sp.lower_val(freed(s)), sp.lower_val(landed(s))
                if e := back(s, 0):
                    sp.wait_ge(a_xn, freed(e))
                    sp.wait_ge(a_xb, freed(e))
                    sp.dma_start(x_sb[:, e.u, :], x_t[e.t, :, :]).then_inc(a_in[e.u], 16)
                if e := back(s, 1):
                    sp.lower_val(done(e)), sp.lower_val(e.t)
                    sp.wait_ge(a_xb, done(e))
                    sp.dma_start(xb_t[e.t, :, :], x2[:, e.u, :]).then_inc(a_xbo[e.u], 16)

            sweep(sp, 1, load_a)
            for t, a in ((wqT_sb, wqT), (wproj_sb, wproj), (wg2_sb, wg2), (br_sb, br), (wr_sb, wr),
                         (flng_sb, flng), (flnb_sb, flnb), (b1_sb, b1), (edges_i, edges)):
                sp.dma_start(t if isinstance(t, bass.AP) else t[:], a).then_inc(s_wb, 16)
            def rows_b(s):
                sp.lower_val(s.t), sp.lower_val(freed(s)), sp.lower_val(s.i)
                if e := back(s, 0):
                    sp.wait_ge(b_x2, freed(e))
                    sp.dma_start(x_sb[:, e.u, :], xb_t[e.t, :, :]).then_inc(b_in[e.u], 16)
                if e := back(s, 2):
                    sp.lower_val(done(e)), sp.lower_val(e.t)
                    sp.wait_ge(b_x2, done(e))
                    sp.dma_start(out_t[e.t, :, :], x2[:, e.u, :]).then_inc(b_x2o[e.u], 16)
                if e := back(s, 5):
                    sp.lower_val(done(e)), sp.lower_val(e.t)
                    sp.wait_ge(b_x4, done(e))
                    sp.dma_start(x4_t[e.t, :, :], x4[:, e.u, :]).then_inc(b_x4o[e.u], 16)

            sp.wait_ge(a_xn, NT + 2)
            for u in range(2):
                sp.wait_ge(a_xbo[u], 16 * (NT // 2 + 1))
            sweep(sp, 5, rows_b)
            sp.wait_ge(s_ctx, 1)
            sp.dma_start(w1_all, w1).then_inc(s_w1, 16)
            sp.dma_start(b2_all, b2).then_inc(s_b2, 16)
            sp.wait_ge(b_omm, NT + 2)
            sp.wait_ge(b_hgb, NT + 2)
            sp.dma_start(w2_all[:, :], w2).then_inc(s_w2, 16)
            sp.dma_start(out[NP:NP + P, :], zrow[:, :]).then_inc(s_dummy, 16)
            sp.wait_ge(s_dummy, 16)
            sp.wait_ge(f_add, 16 * FT)
            for u in range(2):
                sp.wait_ge(b_x2o[u], 16 * (NT // 2 + 1))
                sp.wait_ge(b_x4o[u], 16 * (NT // 2 + 1))

        @block.gpsimd
        def _(pool):
            for s, start in at_start.values():
                if start:
                    pool.sem_inc(s, start)
            nc.gpsimd.memset(ones[:, :], 1.0).then_inc(s_pool, 1)
            nc.gpsimd.memset(ident[:, :], 0.0).then_inc(s_pool, 1)
            nc.gpsimd.iota(cols[:, :], pattern=[[1, P]], base=0, channel_multiplier=0,
                           allow_small_or_imprecise_dtypes=True).then_inc(s_pool, 1)
            nc.gpsimd.iota(desc[:, :], pattern=[[-1, NE]], base=NE, channel_multiplier=0,
                           allow_small_or_imprecise_dtypes=True).then_inc(s_pool, 1)
            nc.gpsimd.iota(dummy[:, :], pattern=[[0, 1]], base=NP + 1, channel_multiplier=1,
                           allow_small_or_imprecise_dtypes=True).then_inc(s_pool, 1)
            nc.gpsimd.memset(ctx_bd[:, :, :], 0.0).then_inc(s_pool, 1)
            nc.gpsimd.memset(zrow[:, :], 0.0).then_inc(s_pool, 1)
            for at in (C, KV - 1):
                nc.gpsimd.memset(kv_all.rearrange("p (t c) -> p t c", c=KV)[:, :, at:at + 1], 1.0).then_inc(s_pool, 1)
            for j, power_of in enumerate((-0.5, 0.5, -0.5)):
                nc.gpsimd.memset(cexp[:, j:j + 1], power_of).then_inc(s_pool, 1)
            pool.wait_ge(s_pool, 12)
            nc.gpsimd.affine_select(out=ident[:, :], in_=ident[:, :], compare_op=ALU.not_equal, fill=1.0, base=0,
                                    pattern=[[-1, P]], channel_multiplier=1).then_inc(s_pool, 1)
            nc.gpsimd.affine_select(out=upper[:, :], in_=ones[:, :], compare_op=ALU.is_gt, fill=0.0, base=0,
                                    pattern=[[1, P]], channel_multiplier=-1).then_inc(s_pool, 1)

            def power(s, va_sem, s_out, freed_by):
                pool.wait_ge(va_sem, done(s))
                pool.wait_ge(freed_by, freed(s))
                nc.gpsimd.tensor_tensor(rs[:, s.u, :], va[:, s.u, :], cexp[:, :], ALU.pow).then_inc(s_out, 1)

            def step_a(s):
                if back(s, 0):
                    pool.wait_ge(a_in[s.u], landed(s))
                    pool.wait_ge(a_xbo[s.u], left(s))
                    nc.gpsimd.tensor_tensor(x2[:, s.u, :], x_sb[:, s.u, :], bproj_sb[:, :], ALU.add).then_inc(a_xb, 1)
                if back(s, 0):
                    pool.wait_ge(a_r2, freed(s))
                    power(s, a_va, a_pow, a_xn)
                if e := back(s, 1):
                    pool.wait_ge(a_pow, done(e))
                    pool.wait_ge(a_hg, freed(e))
                    nc.gpsimd.tensor_tensor(r2[:, e.u, :], rs[:, e.u, 1:2], rs[:, e.u, 2:3], ALU.mult).then_inc(a_r2, 1)

            pool.wait_ge(s_w, 8 * 16)
            sweep(pool, 1, step_a)
            pool.wait_ge(a_kvc, NT + 2)
            pool.wait_ge(a_most, LAST + 3)
            last_k = kv_all[:, LAST * KV:LAST * KV + C]
            nc.gpsimd.affine_select(out=last_k, in_=last_k, compare_op=ALU.is_gt, fill=-1e30, base=N - LAST * P,
                                    pattern=[[0, C]], channel_multiplier=-1).then_inc(s_pad, 1)
            for t in range(LAST + 1, NT):
                nc.gpsimd.memset(kv_all[:, t * KV:t * KV + C], -1e30).then_inc(s_pad, 1)
            pool.wait_ge(s_ctx, 1)
            pool.wait_ge(s_wb, 9 * 16)
            for u in range(2):
                pool.wait_ge(a_tab[u], 32 * (NT // 2 + 1))

            def step_b(s):
                if e := back(s, 5):
                    power(e, b_va, b_rstd, b_r2)
                if e := back(s, 0):
                    w = e.w
                    if not (isinstance(e.t, int) and e.t < 4):
                        pool.wait_ge(b_gn, e.t - 1)
                    nc.gpsimd.tensor_copy(idx[:, 2 * w:2 * w + 2], edges_i[:, ds(e.t * 2, 2)]).then_inc(b_idx, 1)
                    pool.wait_ge(b_idx, done(e))
                    pool.sem_inc(s_held[2], 1)
                    nc.gpsimd.indirect_dma_start(out=xt_rows[:, w, :], out_offset=None, in_=xt_table,
                                                 in_offset=bass.IndirectOffsetOnAxis(ap=idx[:, 2 * w:2 * w + 1], axis=0)
                                                 ).then_inc(b_gat[w], 16)
                    nc.gpsimd.indirect_dma_start(out=g2[:, w, :], out_offset=None, in_=al_table,
                                                 in_offset=bass.IndirectOffsetOnAxis(ap=idx[:, 2 * w + 1:2 * w + 2], axis=0)
                                                 ).then_inc(b_gat[w], 16)

            sweep(pool, 5, step_b, by=8)

            pool.wait_ge(b_omm, NT + 2)
            pool.wait_ge(b_pmm, NT + 2)
            nc.gpsimd.iota(tok[:, 0, :], pattern=[[P, NT]], base=0, channel_multiplier=1,
                           allow_small_or_imprecise_dtypes=True).then_inc(s_pool, 1)

            pool.wait_ge(s_slots, 1)
            for u in range(2):
                pool.wait_ge(b_x2o[u], 16 * (NT // 2 + 1))
                pool.wait_ge(b_x4o[u], 16 * (NT // 2 + 1))
            pool.wait_ge(s_dummy, 16)

            def gather(t):
                pool.wait_ge(f_x, t + 1)
                nc.gpsimd.tensor_copy(idx[:, 0:1], gidx[:, ds(t, 1)]).then_inc(f_gi, 1)
                pool.wait_ge(f_gi, t + 2)
                pool.sem_inc(s_held[2], 1)
                nc.gpsimd.indirect_dma_start(out=xs, out_offset=None, in_=x4_table,
                                             in_offset=bass.IndirectOffsetOnAxis(ap=idx[:, 0:1], axis=0)
                                             ).then_inc(f_gat, 16)

            def add(t, u):
                if not (isinstance(t, int) and t == 0):
                    pool.wait_ge(f_add, 16 * t)
                nc.gpsimd.tensor_copy(idx[:, 1:2], sidx[:, ds(t, 1)]).then_inc(f_si, 1)
                pool.wait_ge(f_si, t + 2)
                pool.wait_ge(f_yw, t + 2)
                pool.sem_inc(s_held[2], 1)
                nc.gpsimd.indirect_dma_start(out=out, out_offset=bass.IndirectOffsetOnAxis(ap=idx[:, 1:2], axis=0),
                                             in_=yw[:, u, :], in_offset=None, compute_op=ALU.add).then_inc(f_add, 16)

            for t in range(3):
                gather(t)
            with pool.Fori(1, FT // 2) as i:
                gather(2 * i + 1)
                add(2 * i - 2, 0)
                gather(2 * i + 2)
                add(2 * i - 1, 1)
            for t in range(FT - 3, FT):
                add(t, t % 2)

        @block.scalar
        def _(act):
            def step_a(s):
                if e := back(s, 3):
                    u = e.u
                    act.wait_ge(a_row, done(e))
                    act.dma_start(xt_t[e.t, :, :], xt_sb[:, u, :]).then_inc(a_tab[u], 16)
                    act.dma_start(al_t[e.t, :, :], xt_sb[:, u, C:C + HG]).then_inc(a_tab[u], 16)
                    act.wait_ge(a_hg, done(e))
                    nc.scalar.activation(hg_all[:, ds(e.t * GH, GH)], hgpre[:, u, :], ACT.Gelu).then_inc(a_gelu, 1)
                if back(s, 0):
                    act.wait_ge(a_tr, done(s))
                    act.wait_ge(a_gmm, freed(s))
                    nc.scalar.copy(xnT[:, s.u, :], bank[s.u][:, 0:C]).then_inc(a_xnT, 1)
                if e := back(s, 1):
                    act.wait_ge(a_kvmm, done(e))
                    nc.scalar.copy(kv_all[:, ds(e.t * KV, 2 * (C + 1))].rearrange("p (j c) -> p j c", j=2)[:, :, 0:C],
                                   bank[2 + e.u][:, :].rearrange("p (j c) -> p j c", j=2)).then_inc(a_kvc, 1)
                if e := back(s, 0):
                    nc.scalar.copy(xnT_all.rearrange("p (k n) -> p k n", k=NK)[:, :, ds(e.t * P, P)],
                                   bank[e.u][:, 0:C].rearrange("p (k n) -> p k n", k=NK)).then_inc(a_all, 1)

            sweep(act, 3, step_a)
            def step_k(s):
                act.wait_ge(k_sub, done(s))
                act.wait_ge(k_mm, freed(s))
                nc.scalar.activation(ek[:, s.u, :], kd[:, s.u, :], ACT.Exp).then_inc(k_exp, 1)

            sweep(act, 0, step_k, NT // 2)
            act.wait_ge(s_m1, 1)
            nc.scalar.copy(m1[:, :, :].rearrange("p k c -> p (k c)"), bank[4][:, 0:NK * C]).then_inc(s_m1c, 1)

            act.wait_ge(a_gelu, NT + 2)
            act.wait_ge(s_half, 2)

            def step_b(s):
                if e := back(s, 8):
                    act.wait_ge(b_lmm, done(e))
                    nc.scalar.copy(logits[:, ds(e.t * NE, NE)], bank[6 + e.u][:, C:C + NE]).then_inc(b_lc, 1)
                if e := back(s, 2):
                    act.wait_ge(b_alpha, done(e))
                    act.wait_ge(b_gn, freed(e))
                    nc.scalar.activation(sm[:, e.u, :], lg[:, e.u, HG:2 * HG], ACT.Exp, bias=lg[:, e.u, 2 * HG:2 * HG + 1],
                                         accum_out=lg[:, e.u, 2 * HG + 1:2 * HG + 2]).then_inc(b_exp, 1)
                if e := back(s, 0):
                    act.wait_ge(b_htr, freed(e))
                    nc.scalar.copy(hgb[:, e.u, :], hg_all[:, ds(e.t * GH, GH)]).then_inc(b_hgb, 1)
                if e := back(s, 2):
                    act.wait_ge(b_exp, done(e))
                    act.wait_ge(b_x2, freed(e))
                    nc.scalar.activation(tmp[:, e.u, :], xt_rows[:, e.w, 0:DG], ACT.Copy, scale=sm[:, e.u, 0:1]).then_inc(b_g0, 1)
                if e := back(s, 2):
                    act.wait_ge(b_gmm, done(e))
                    act.wait_ge(b_og, freed(e))
                    for f in range(NK):
                        last = nc.scalar.activation(sg[:, e.u, f * P:(f + 1) * P], bank[2 + e.u][:, P * (f + 1):P * (f + 2)],
                                                    ACT.Tanh, bias=vec[:, 2, f:f + 1], scale=0.5)
                    last.then_inc(b_sg, 1)
                if e := back(s, 1):
                    act.wait_ge(b_htr, done(e))
                    act.wait_ge(b_gmm, freed(e))
                    nc.scalar.copy(hgT[0:GH, e.u, :], bank[2 + e.u][0:GH, 0:P]).then_inc(b_hgT, 1)
                if e := back(s, 6):
                    act.wait_ge(b_x3, done(e))
                    act.wait_ge(b_r2, done(e))
                    act.wait_ge(b_x4o[e.u], left(e))
                    nc.scalar.activation(x4[:, e.u, :], xn[:, e.u, :], ACT.Copy, scale=r2[:, e.u, :]).then_inc(b_x4, 1)
                    act.wait_ge(b_tr, done(e))
                    act.wait_ge(b_lmm, freed(e))
                    nc.scalar.copy(xnT[:, e.u, :], bank[6 + e.u][:, 0:C]).then_inc(b_xnT, 1)

            sweep(act, 8, step_b, by=8)

            act.wait_ge(s_diff, 1)
            nc.scalar.activation(tok[:, 4, :], tok[:, 3, :], ACT.Exp).then_inc(s_exp, 1)

            act.wait_ge(s_low, 1)

            def distance(i, n):
                b = n % 4
                act.wait_ge(t_mm, 2 * TURN * i + n + 1)
                nc.scalar.activation(far[:, b, :], cols[:, 0:FT], ACT.Abs, scale=-1.0,
                                     bias=tok[:, 12 + 2 * (n % 2), ds(TURN * i + n // 2, 1)]).then_inc(t_far[b], 1)

            def weight(i, n):
                b, at = n % 4, ds(TURN * i + n // 2, 1)
                act.wait_ge(t_far[b], TURN // 2 * i + n // 4 + 2)
                nc.scalar.activation(rv[:, b, FT:2 * FT], far[:, b, :], ACT.Relu, scale=tok[:, 9 + n % 2, at],
                                     bias=tok[:, 5 + n % 2, at]).then_inc(t_w[b], 1)

            with act.Fori(0, NT // TURN) as i:
                for n in range(0, 2 * TURN, 4):
                    distance(i, n)
                    distance(i, n + 1)
                    weight(i, n)
                    distance(i, n + 2)
                    weight(i, n + 1)
                    weight(i, n + 2)
            act.wait_ge(s_slots, 1)

            def w1_chunk(t, u, e):
                if not (isinstance(t, int) and t < 2):
                    act.wait_ge(f_h, t)
                nc.scalar.copy(w1_tile[:, u, 0:HID], w1_all[:, ds(e * (NK * HID), HID)]).then_inc(f_w1[0], 1)

            def rows(t, u, e):
                act.wait_ge(f_x, t + 2)
                for k in range(NK):
                    last = nc.scalar.activation(xsT[:, u, k * P:(k + 1) * P], bank[0][:, k * P:(k + 1) * P], ACT.Identity,
                                                scale=flng_sb[:, ds(e + k * NE, 1)], bias=flnb_sb[:, ds(e + k * NE, 1)])
                last.then_inc(f_xe, 1)

            def gelu(t, u, e):
                act.wait_ge(f_h, t + 2)
                if not (isinstance(t, int) and t < 2):
                    act.wait_ge(f_y, t)
                for c in range(2 * HC):
                    last = nc.scalar.activation(hidT[:, u, c * P:(c + 1) * P], bank[4 + 2 * u + c // HC][:, ds(c % HC * P, P)],
                                                ACT.Gelu, bias=b1_sb[:, ds(e * (2 * HC) + c, 1)])
                last.then_inc(f_ge, 1)

            def expert(t):
                return act.value_load(te[0:1, ds(t, 1)], min_val=0, max_val=NE - 1)

            def step_f(t, u, last=False):
                if not last:
                    e = expert(t + 1)
                    w1_chunk(t + 1, 1 - u, e)
                    rows(t + 1, 1 - u, e)
                gelu(t, u, expert(t))

            act.wait_ge(s_w1, 16)
            act.wait_ge(s_wb, 9 * 16)
            w1_chunk(0, 0, expert(0))
            rows(0, 0, expert(0))
            step_f(0, 0)
            step_f(1, 1)
            with act.Fori(1, FT // 2) as i:
                step_f(2 * i, 0)
                step_f(2 * i + 1, 1)
            step_f(FT - 1, 0, last=True)

        @block.vector
        def _(dve):
            chained = [0]

            def link(ins):
                chained[0] += 1
                ins.then_inc(s_r, 1)
                dve.wait_ge(s_r, chained[0])

            dve.wait_ge(s_w, 8 * 16)
            dve.wait_ge(s_pool, 14)
            nc.vector.tensor_scalar(vec[:, 2, :], vec[:, 2, :], 0.5, None, ALU.mult).then_inc(s_half, 1)
            for k in range(NK):
                for s in range(2):
                    link(nc.vector.tensor_tensor(sg[:, 0, :], wm[:, k, 2 * C:3 * C], attn_sb[:, s, :], ALU.mult))
                    link(nc.vector.tensor_reduce(wm[:, k, 3 * C + s * HG:3 * C + (s + 1) * HG],
                                                 sg[:, 0, :].rearrange("p (h d) -> p h d", h=HG), AX.X, ALU.add))
            for k in range(NK):
                nc.vector.tensor_copy(R3[:, 512 + k * P:512 + (k + 1) * P],
                                      vec[:, 1, k:k + 1].to_broadcast([P, P])).then_inc(s_lnb, 1)
            dve.wait_ge(s_bg, 1)
            nc.vector.tensor_tensor(bg1_sb[:, :], bg1_sb[:, :], bank[0][:, 0:GH], ALU.add).then_inc(s_prep, 1)
            for k in range(NK):
                nc.vector.tensor_scalar(wm[:, k, 2 * C + ROW:WM], wm[:, k, 2 * C + ROW:WM], vec[:, 0, k:k + 1], None,
                                        ALU.mult).then_inc(s_prep, 1)
            dve.wait_ge(s_prep, 1 + NK)

            def variances(s, mv_sem, s_out):
                u = s.u
                dve.wait_ge(mv_sem, done(s))
                nc.vector.tensor_scalar(va[:, u, 0:2], mv[:, u, 1:2].to_broadcast([P, 2]), EPS, None, ALU.add)
                nc.vector.tensor_scalar(va[:, u, 2:3], mv[:, u, 1:2], 1.0 + EPS, EPS * EPS, ALU.mult, ALU.add
                                        ).then_inc(s_out, 1)

            nc.vector.memset(k_most, -BIG).then_inc(s_most, 1)
            dve.wait_ge(s_most, 1)

            def stats_a(s):
                u = s.u
                dve.wait_ge(a_in[u], landed(s))
                nc.vector.bn_stats(st[:, u, :], x_sb[:, u, :]).then_inc(a_stats, 1)
                dve.wait_ge(a_stats, done(s))
                dve.wait_ge(a_pow, freed(s))
                dve.sem_inc(s_held[0], 1)
                nc.vector.bn_aggr(mv[:, u, :], st[:, u, :]).then_inc(a_mv, 1)
                variances(s, a_mv, a_va)

            def norm_a(s):
                u = s.u
                dve.wait_ge(a_pow, done(s))
                dve.wait_ge(a_tr, freed(s))
                nc.vector.tensor_scalar(xn[:, u, :], x_sb[:, u, :], mv[:, u, 0:1], rs[:, u, 0:1],
                                        ALU.subtract, ALU.mult).then_inc(a_xn, 1)

            def take_a(s):
                u = s.u
                dve.wait_ge(a_kvc, done(s))
                rows = P if not isinstance(s.t, int) else min(P, max(0, N - s.t * P))
                if rows:
                    dve.wait_ge(a_most, done(s) - 1)
                    nc.vector.tensor_tensor(k_most[0:rows, :], k_most[0:rows, :], kv_all[0:rows, ds(s.t * KV, C)],
                                            ALU.max).then_inc(a_most, 1)
                dve.wait_ge(a_gmm, done(s))
                dve.wait_ge(a_tab[u], left(s, 32))
                nc.vector.tensor_copy(xt_sb[:, u, :], bank[6 + u][:, 0:ROW]).then_inc(a_row, 1)
                dve.wait_ge(a_gelu, freed(s))
                dve.wait_ge(a_r2, done(s))
                nc.vector.scalar_tensor_tensor(out=hgpre[:, u, :], in0=bank[6 + u][:, ROW:ROW + GH], scalar=r2[:, u, :],
                                               in1=bg1_sb[:, :], op0=ALU.mult, op1=ALU.add).then_inc(a_hg, 1)

            def step_a(s):
                if e := back(s, 1):
                    norm_a(e)
                if back(s, 0):
                    stats_a(s)
                if e := back(s, 3):
                    take_a(e)

            sweep(dve, 3, step_a)
            dve.wait_ge(s_most, 2)
            nc.vector.tensor_reduce(k_col[:, :], bank[0][:, 0:C].rearrange("p (k n) -> p k n", k=NK), AX.X, ALU.max
                                    ).then_inc(s_col, 1)
            dve.wait_ge(s_col, 1)
            nc.vector.tensor_copy(k_wide.rearrange("p (k n) -> p k n", k=NK),
                                  k_col[:, :].unsqueeze(2).to_broadcast([P, NK, P])).then_inc(s_wide, 1)
            dve.wait_ge(s_krow, 1)
            nc.vector.tensor_copy(k_row, bank[1][:, 0:C]).then_inc(s_krow, 1)
            dve.wait_ge(s_krow, 2)
            dve.wait_ge(s_pad, NT - LAST)

            def step_k(s):
                dve.wait_ge(k_exp, freed(s))
                nc.vector.tensor_tensor(kd[:, s.u, :].rearrange("p (j c) -> p j c", j=2),
                                        kv_all[:, ds(s.t * (2 * KV), 2 * KV)].rearrange("p (j c) -> p j c", j=2)[:, :, 0:C],
                                        k_row.unsqueeze(1).to_broadcast([P, 2, C]), ALU.subtract).then_inc(k_sub, 1)

            sweep(dve, 0, step_k, NT // 2)
            dve.wait_ge(s_wb, 9 * 16)
            nc.vector.tensor_scalar(wproj_sb[:, :, :], wproj_sb[:, :, :], 0.5, None, ALU.mult).then_inc(s_half, 1)
            dve.wait_ge(s_csum, 1)
            for f in range(NK):
                link(nc.vector.reciprocal(kinv[:, f:f + 1], bank[2 + f][:, f * P:f * P + 1]))
            for f in range(NK):
                for h in range(P // DM):
                    r = slice(h * DM, (h + 1) * DM)
                    at = 1 - f + h * DM
                    ins = nc.vector.tensor_scalar(ctx_bd[r, f, r], bank[2 + f][r, at:at + DM], kinv[r, f:f + 1], None, ALU.mult)
            ins.then_inc(s_ctx, 1)

            def mix_b(e):
                dve.wait_ge(b_pmm, done(e))
                dve.wait_ge(b_in[e.u], landed(e))
                nc.vector.tensor_tensor(x_sb[:, e.u, :], bank[4 + e.u][:, 0:C], x_sb[:, e.u, :], ALU.add).then_inc(b_mix, 1)

            def x2_b(e):
                dve.wait_ge(b_mix, done(e))
                dve.wait_ge(b_x2o[e.u], left(e))
                dve.wait_ge(b_gn, done(e))
                nc.vector.scalar_tensor_tensor(out=x2[:, e.u, :].rearrange("p (h d) -> p h d", h=HG),
                                               in0=tmp[:, e.u, :].unsqueeze(1).to_broadcast([P, HG, DG]),
                                               scalar=lg[:, e.u, 10:11],
                                               in1=x_sb[:, e.u, :].rearrange("p (h d) -> p h d", h=HG),
                                               op0=ALU.mult, op1=ALU.add).then_inc(b_x2, 1)

            def stats_b(e):
                dve.wait_ge(b_x2, done(e))
                nc.vector.bn_stats(st[:, e.u, :], x2[:, e.u, :]).then_inc(b_stats, 1)

            def aggr_b(e):
                dve.wait_ge(b_stats, done(e))
                dve.wait_ge(b_rstd, freed(e))
                dve.sem_inc(s_held[0], 1)
                nc.vector.bn_aggr(mv[:, e.u, :], st[:, e.u, :]).then_inc(b_mv, 1)

            def alpha_b(e):
                dve.wait_ge(b_gat[e.w], e.q * 32 + 32)
                dve.wait_ge(b_exp, freed(e))
                nc.vector.tensor_tensor(lg[:, e.u, 0:HG], g2[:, e.w, :], xt_rows[:, e.w, C + HG:ROW], ALU.add).then_inc(b_al, 1)

            def leaky_b(e):
                dve.wait_ge(b_al, done(e))
                nc.vector.scalar_tensor_tensor(out=lg[:, e.u, HG:2 * HG], in0=lg[:, e.u, 0:HG], scalar=0.01,
                                               in1=lg[:, e.u, 0:HG], op0=ALU.mult, op1=ALU.max).then_inc(b_lk, 1)

            def most_b(e):
                dve.wait_ge(b_lk, done(e))
                nc.vector.tensor_reduce(lg[:, e.u, 8:9], lg[:, e.u, HG:2 * HG], AX.X, ALU.max, negate=True
                                        ).then_inc(b_alpha, 1)

            def gate_b(e):
                dve.wait_ge(b_omm, done(e))
                dve.wait_ge(b_sg, done(e))
                dve.wait_ge(b_pmm, freed(e))
                nc.vector.scalar_tensor_tensor(out=og[:, e.u, :], in0=sg[:, e.u, :], scalar=1.0, in1=bank[e.u][:, 0:C],
                                               op0=ALU.add, op1=ALU.mult).then_inc(b_og, 1)

            def head_b(e, h, before, after):
                dve.wait_ge(before, done(e))
                if h == 1:
                    nc.vector.reciprocal(lg[:, e.u, 10:11], lg[:, e.u, 9:10])
                nc.vector.scalar_tensor_tensor(out=tmp[:, e.u, :], in0=xt_rows[:, e.w, h * DG:(h + 1) * DG],
                                               scalar=sm[:, e.u, h:h + 1], in1=tmp[:, e.u, :],
                                               op0=ALU.mult, op1=ALU.add).then_inc(after, 1)

            def norm_b(e):
                u = e.u
                dve.wait_ge(b_rstd, done(e))
                dve.wait_ge(b_tr, freed(e))
                dve.wait_ge(b_x4, freed(e))
                nc.vector.tensor_scalar(xn[:, u, :], x2[:, u, :], mv[:, u, 0:1], rs[:, u, 0:1],
                                        ALU.subtract, ALU.mult).then_inc(b_x3, 1)
                nc.vector.tensor_tensor(r2[:, u, :], rs[:, u, 1:2], rs[:, u, 2:3], ALU.mult).then_inc(b_r2, 1)

            def step_b(s):
                e1, e2, e3, e5 = (back(s, lag) for lag in (1, 2, 3, 5))
                if e5:
                    norm_b(e5)
                if e2:
                    head_b(e2, 1, b_g0, b_g1)
                if e3:
                    mix_b(e3)
                if e1:
                    alpha_b(e1)
                if e2:
                    head_b(e2, 2, b_g1, b_g2)
                if e3:
                    x2_b(e3)
                if e1:
                    leaky_b(e1)
                if e2:
                    gate_b(e2)
                if e3:
                    stats_b(e3)
                if e1:
                    most_b(e1)
                if e2:
                    head_b(e2, 3, b_g2, b_gn)
                if e3:
                    aggr_b(e3)
                    variances(e3, b_mv, b_va)

            sweep(dve, 5, step_b, by=8)

            dve.wait_ge(b_lc, NT + 2)
            dve.wait_ge(s_pool, 15)
            for u in range(2):
                dve.wait_ge(b_x2o[u], 16 * (NT // 2 + 1))
                dve.wait_ge(b_x4o[u], 16 * (NT // 2 + 1))
            te3 = lambda a: a.rearrange("p (t e) -> p t e", e=NE)
            wide = lambda a: a.unsqueeze(2).to_broadcast([P, NT, NE])
            desc3 = desc[:, :].unsqueeze(1).to_broadcast([P, NT, NE])
            TOK, M, D, DIFF, EXP, W, SLOT = 0, 1, 2, 3, 4, 5, 7
            link(nc.vector.tensor_tensor(te3(logits), te3(logits), br_sb[:, :].unsqueeze(1).to_broadcast([P, NT, NE]), ALU.add))
            for k in range(2):
                of = work if k else logits
                m, d = tok[:, 9 + k, :], tok[:, D, :]
                link(nc.vector.tensor_reduce(m, te3(of), AX.X, ALU.max))
                link(nc.vector.tensor_tensor(te3(chosen), te3(of), wide(m), ALU.is_equal))
                link(nc.vector.tensor_tensor(te3(chosen), te3(chosen), desc3, ALU.mult))
                link(nc.vector.tensor_reduce(d, te3(chosen), AX.X, ALU.max))
                link(nc.vector.tensor_tensor(te3(oh[k]), desc3, wide(d), ALU.is_equal))
                if k == 0:
                    link(nc.vector.scalar_tensor_tensor(out=work, in0=oh[0], scalar=-BIG, in1=logits,
                                                        op0=ALU.mult, op1=ALU.add))
            link(nc.vector.tensor_scalar(tok[:, M, :], tok[:, TOK, :], float(N), None, ALU.is_lt))
            link(nc.vector.tensor_tensor(chosen, oh[0], oh[1], ALU.add))
            link(nc.vector.tensor_tensor(te3(chosen), te3(chosen), wide(tok[:, M, :]), ALU.mult))
            nc.vector.tensor_tensor(tok[:, DIFF, :], tok[:, 10, :], tok[:, 9, :], ALU.subtract).then_inc(s_diff, 1)
            dve.sem_inc(s_chosen, 1)
            dve.wait_ge(s_exp, 1)
            link(nc.vector.tensor_scalar(tok[:, D, :], tok[:, EXP, :], 1.0, None, ALU.add))
            link(nc.vector.reciprocal(tok[:, W, :], tok[:, D, :]))
            link(nc.vector.tensor_tensor(tok[:, W + 1, :], tok[:, EXP, :], tok[:, W, :], ALU.mult))
            link(nc.vector.tensor_scalar(tok[:, 9:11, :], tok[:, W:W + 2, :], -1.0, None, ALU.mult))
            dve.wait_ge(s_tot, 1)
            nc.vector.tensor_copy(ttb[0:NT, :].rearrange("p (e c) -> p e c", e=NE),
                                  bank[0][0:NT, 0:NE].unsqueeze(2).to_broadcast([NT, NE, P])).then_inc(s_ttb, 1)
            dve.wait_ge(s_pos, 1)
            link(nc.vector.tensor_copy(pos, bank[1][:, 0:NE * (NT + 1)]))
            pos3 = pos.rearrange("p (e t) -> p e t", e=NE)
            size, base, end = small[:, :], bounds[:, 0:NE], bounds[:, 1:NE + 1]
            link(nc.vector.tensor_scalar(small_i[:, 0, :], pos3[:, :, NT], float(P - 1), None, ALU.add))
            link(nc.vector.tensor_scalar(small_i[:, 1, :], small_i[:, 0, :], -P, None, ALU.bitwise_and))
            link(nc.vector.tensor_copy(size, small_i[:, 1, :]))
            link(nc.vector.memset(bounds[:, 0:1], 0.0))
            for e in range(NE):
                link(nc.vector.tensor_tensor(bounds[:, e + 1:e + 2], bounds[:, e:e + 1], size[:, e:e + 1], ALU.add))
            pos_te = pos3[:, :, 0:NT]
            link(nc.vector.tensor_tensor(pos_te, pos_te, base.unsqueeze(2).to_broadcast([P, NE, NT]), ALU.add))
            link(nc.vector.tensor_scalar(tok[:, D, :], tok[:, M, :], -1000.0, 1000.0, ALU.mult, ALU.add))
            for k in range(2):
                slot = tok[:, SLOT + k, :]
                link(nc.vector.tensor_tensor(te3(work), te3(oh[k]), pos_te.rearrange("p e t -> p t e"), ALU.mult))
                link(nc.vector.tensor_reduce(slot, te3(work), AX.X, ALU.add))
                si, lo, hi = (tok_i[:, 3 * k + j, :] for j in range(3))
                link(nc.vector.tensor_copy(si, slot))
                link(nc.vector.tensor_scalar(lo, si, P - 1, None, ALU.bitwise_and))
                link(nc.vector.tensor_scalar(hi, si, 7, None, ALU.logical_shift_right))
                link(nc.vector.tensor_copy(tok[:, 11 + 2 * k, :], lo))
                link(nc.vector.tensor_tensor(tok[:, 11 + 2 * k, :], tok[:, 11 + 2 * k, :], tok[:, D, :], ALU.add))
                link(nc.vector.tensor_copy(tok[:, 12 + 2 * k, :], hi))
            link(nc.vector.tensor_scalar(tok[:, DIFF, :], tok[:, TOK, :], 1.0, None, ALU.add))

            dve.sem_inc(s_low, 1)

            def onehots(s, b, k, t):
                dve.wait_ge(t_mm, s + 1)
                nc.vector.tensor_scalar(ohb[:, b, :], cols[:, :], tok[:, 11 + 2 * k, ds(t, 1)], None,
                                        ALU.is_equal).then_inc(t_oh, 1)
                nc.vector.tensor_scalar(rv[:, b, 0:FT], cols[:, 0:FT], tok[:, 12 + 2 * k, ds(t, 1)],
                                        tok[:, DIFF, ds(t, 1)], ALU.is_equal, ALU.mult).then_inc(t_idx, 1)
                if b == 3:
                    nc.vector.tensor_scalar(rv[:, b, FT:2 * FT], cols[:, 0:FT], tok[:, 12 + 2 * k, ds(t, 1)],
                                            tok[:, W + k, ds(t, 1)], ALU.is_equal, ALU.mult).then_inc(t_w[b], 1)

            with dve.Fori(0, NT // TURN) as i:
                for n in range(2 * TURN):
                    onehots(2 * TURN * i + n, n % 4, n % 2, TURN * i + n // 2)
            link(nc.vector.tensor_scalar(sl[:, 0, :], cols[:, 0:FT], float(P), None, ALU.mult))
            link(nc.vector.tensor_scalar(sl[:, 1, :], sl[:, 0, :], end[:, 0:1], None, ALU.is_ge))
            for e in range(1, NE - 1):
                link(nc.vector.scalar_tensor_tensor(out=sl[:, 1, :], in0=sl[:, 0, :], scalar=end[:, e:e + 1],
                                                    in1=sl[:, 1, :], op0=ALU.is_ge, op1=ALU.add))
            link(nc.vector.tensor_copy(te, sl[0:1, 1, :]))
            dve.wait_ge(s_table, 1)
            link(nc.vector.tensor_scalar(sl[:, 0, :], bank[2][:, 0:FT], 1.0, None, ALU.subtract))
            link(nc.vector.tensor_copy(slot_w, bank[2][:, FT:2 * FT]))
            link(nc.vector.tensor_scalar(gidx, sl[:, 0, :], 0.0, None, ALU.max))
            link(nc.vector.tensor_scalar(sl[:, 1, :], sl[:, 0, :], 0.0, None, ALU.is_lt))
            nc.vector.scalar_tensor_tensor(out=sidx, in0=sl[:, 1, :], scalar=dummy[:, 0:1], in1=sl[:, 0, :],
                                           op0=ALU.mult, op1=ALU.add).then_inc(s_slots, 1)

            dve.wait_ge(s_w1, 16)
            dve.wait_ge(s_b2, 16)

            def w1_chunk(t, u):
                if not (isinstance(t, int) and t < 2):
                    dve.wait_ge(f_h, t)
                nc.vector.tensor_copy(w1_tile[:, u, HID:2 * HID], w1_all[:, ds(expert(t) * (NK * HID) + HID, HID)]
                                      ).then_inc(f_w1[1], 1)

            def result(t, u):
                dve.wait_ge(f_y, t + 2)
                dve.wait_ge(f_yw, t + 1)
                nc.vector.tensor_tensor(y1, bank[1 + u][:, 0:C], b2_all[:, ds(expert(t) * C, C)], ALU.add).then_inc(f_y1, 1)
                dve.wait_ge(f_y1, t + 2)
                if not (isinstance(t, int) and t < 2):
                    dve.wait_ge(f_add, 16 * t - 16)
                nc.vector.tensor_scalar(yw[:, u, :], y1, slot_w[:, ds(t, 1)], None, ALU.mult).then_inc(f_yw, 1)

            def expert(t):
                return dve.value_load(te[0:1, ds(t, 1)], min_val=0, max_val=NE - 1)

            w1_chunk(0, 0)
            w1_chunk(1, 1)
            w1_chunk(2, 0)
            result(0, 0)
            with dve.Fori(1, FT // 2) as i:
                w1_chunk(2 * i + 1, 1)
                result(2 * i - 1, 1)
                w1_chunk(2 * i + 2, 0)
                result(2 * i, 0)
            result(FT - 2, 1)
            result(FT - 1, 0)

        @block.tensor
        def _(pe):
            pe.wait_ge(s_lnb, NK)
            for k in range(NK):
                mm = nc.tensor.matmul(bank[0][:, 0:GH], R3[:, 512 + k * P:512 + (k + 1) * P], wm[:, k, 2 * C + ROW:WM],
                                      start=(k == 0), stop=(k == NK - 1))
            mm.then_inc(s_bg, 1)
            pe.wait_ge(s_prep, 1 + NK)

            def turn(out, src, s_out):
                for k in range(NK):
                    mm = nc.tensor.transpose(out[:, k * P:(k + 1) * P], src[:, k * P:(k + 1) * P], ident[:, :])
                mm.then_inc(s_out, 1)

            def project_a(s):
                u = s.u
                pe.wait_ge(a_xnT, done(s))
                pe.wait_ge(a_kvc, freed(s))
                for k in range(NK):
                    mm = nc.tensor.matmul(bank[2 + u][:, :], xnT[:, u, k * P:(k + 1) * P], wm[:, k, 0:2 * C],
                                          start=(k == 0), stop=(k == NK - 1))
                mm.then_inc(a_kvmm, 1)
                pe.wait_ge(a_hg, freed(s))
                for k in range(NK):
                    mm = nc.tensor.matmul(bank[6 + u][:, 0:ROW + GH], xnT[:, u, k * P:(k + 1) * P], wm[:, k, 2 * C:WM],
                                          start=(k == 0), stop=(k == NK - 1))
                mm.then_inc(a_gmm, 1)

            def step_a(s):
                if e := back(s, 0):
                    pe.wait_ge(a_xn, done(e))
                    pe.wait_ge(a_all, freed(e))
                    turn(bank[e.u], xn[:, e.u, :], a_tr)
                if e := back(s, 1):
                    project_a(e)

            sweep(pe, 1, step_a)

            def zeros(outs, **flags):
                for o in outs:
                    mm = nc.tensor.matmul(o, zrow[:, 0:P], zrow[:, 0:o.shape[1]], **flags)
                return mm

            pe.wait_ge(a_most, LAST + 3)
            pe.wait_ge(a_all, NT + 2)
            turn(bank[0], k_most, s_most)
            pe.wait_ge(s_wide, 1)
            turn(bank[1], k_wide, s_krow)

            def step_k(s):
                pe.wait_ge(k_exp, done(s))
                for j in range(2):
                    for f in range(NK):
                        mm = nc.tensor.matmul(bank[2 + f][:, 0:P + 1], ek[:, s.u, j * C + f * P:j * C + (f + 1) * P],
                                              kv_all[:, ds(s.t * (2 * KV) + j * KV + C + f * (P + 1), P + 1)],
                                              start=False, stop=False)
                mm.then_inc(k_mm, 1)

            pe.wait_ge(a_kvc, NT + 2)
            sums = [bank[2][:, 0:P + 1], bank[3][:, 0:P + 1]]
            zeros(sums, start=True, stop=False)
            sweep(pe, 0, step_k, NT // 2)
            zeros(sums, start=False, stop=True).then_inc(s_csum, 1)
            pe.wait_ge(s_wb, 9 * 16)
            pe.wait_ge(s_ctx, 1)
            for k in range(NK):
                for f in range(NK):
                    mm = nc.tensor.matmul(bank[4][:, k * C + f * P:k * C + (f + 1) * P], wqT_sb[:, f, k * P:(k + 1) * P],
                                          ctx_bd[:, f, :], start=True, stop=True)
            mm.then_inc(s_m1, 1)
            pe.wait_ge(s_m1c, 1)
            pe.wait_ge(s_half, 2)

            def step_b(s):
                if e := back(s, 3):
                    pe.wait_ge(b_og, done(e))
                    pe.wait_ge(b_mix, freed(e))
                    for f in range(NK):
                        mm = nc.tensor.matmul(bank[4 + e.u][:, 0:C], og[:, e.u, f * P:(f + 1) * P], wproj_sb[:, f, :],
                                              start=(f == 0), stop=(f == NK - 1))
                    mm.then_inc(b_pmm, 1)
                if e := back(s, 1):
                    pe.wait_ge(b_og, freed(e))
                    for f in range(NK):
                        for k in range(NK):
                            mm = nc.tensor.matmul(bank[e.u][:, f * P:(f + 1) * P], m1[:, k, f * P:(f + 1) * P],
                                                  tile_of(xnT_all, k, e), start=(k == 0), stop=(k == NK - 1))
                    mm.then_inc(b_omm, 1)
                if e := back(s, 6):
                    pe.wait_ge(b_x3, done(e))
                    pe.wait_ge(b_lc, freed(e))
                    turn(bank[6 + e.u], xn[:, e.u, :], b_tr)
                if e := back(s, 0):
                    pe.wait_ge(b_hgb, done(e))
                    pe.wait_ge(b_sg, freed(e))
                    pe.sem_inc(s_held[1], 1)
                    nc.tensor.transpose(bank[2 + e.u][0:GH, 0:P], hgb[:, e.u, :], ident[:, :]).then_inc(b_htr, 1)
                if e := back(s, 7):
                    pe.wait_ge(b_xnT, done(e))
                    for k in range(NK):
                        mm = nc.tensor.matmul(bank[6 + e.u][:, C:C + NE], xnT[:, e.u, k * P:(k + 1) * P], wr_sb[:, k, :],
                                              start=(k == 0), stop=(k == NK - 1))
                    mm.then_inc(b_lmm, 1)
                if e := back(s, 1):
                    pe.wait_ge(b_hgT, done(e))
                    for f in range(NK):
                        mm = nc.tensor.matmul(bank[2 + e.u][:, (f + 1) * P:(f + 2) * P], wg2_sb[:, f * P:(f + 1) * P],
                                              hgT[0:GH, e.u, :], start=True, stop=True)
                    mm.then_inc(b_gmm, 1)

            sweep(pe, 7, step_b, by=8)

            pe.wait_ge(s_chosen, 1)
            ch3 = chosen.rearrange("p (t e) -> p t e", e=NE)
            for e in range(NE):
                mm = nc.tensor.matmul(bank[0][0:NT, e:e + 1], ch3[:, :, e], ones[:, 0:1], start=True, stop=True)
            mm.then_inc(s_tot, 1)
            pe.wait_ge(s_ttb, 1)
            for e in range(NE):
                at = e * (NT + 1)
                nc.tensor.matmul(bank[1][:, at:at + NT + 1], ttb[0:NT, e * P:(e + 1) * P], upper[0:NT, 0:NT + 1],
                                 start=True, stop=False)
                mm = nc.tensor.matmul(bank[1][:, at:at + NT], upper[:, :], ch3[:, :, e], start=False, stop=True)
            mm.then_inc(s_pos, 1)
            table = bank[2][:, 0:2 * FT]
            zeros([table], start=True, stop=False)
            with pe.Fori(0, NT // TURN) as i:
                for n in range(2 * TURN):
                    s, b = 2 * TURN * i + n, n % 4
                    pe.wait_ge(t_oh, s + 5)
                    pe.wait_ge(t_idx, s + 5)
                    pe.wait_ge(t_w[b], TURN // 2 * i + n // 4 + 2)
                    nc.tensor.matmul(table, ohb[:, b, :], rv[:, b, :], start=False, stop=False).then_inc(t_mm, 1)
            zeros([table], start=False, stop=True).then_inc(s_table, 1)

            def rows(t):
                pe.wait_ge(f_gat, 16 * t + 16)
                pe.wait_ge(f_xe, t + 1)
                turn(bank[0], xs, f_x)

            def hidden(t, u):
                pe.wait_ge(f_xe, t + 2)
                for k in range(NK):
                    pe.wait_ge(f_w1[k], t + 2)
                if not (isinstance(t, int) and t < 2):
                    pe.wait_ge(f_ge, t)
                for c in range(2 * HC):
                    for k in range(NK):
                        mm = nc.tensor.matmul(bank[4 + 2 * u + c // HC][:, c % HC * P:(c % HC + 1) * P],
                                              w1_tile[:, u, k * HID + c * P:k * HID + (c + 1) * P],
                                              xsT[:, u, k * P:(k + 1) * P], start=(k == 0), stop=(k == NK - 1))
                mm.then_inc(f_h, 1)

            def second(t, u):
                e = pe.value_load(te[0:1, ds(t, 1)], min_val=0, max_val=NE - 1)
                pe.wait_ge(f_ge, t + 2)
                if not (isinstance(t, int) and t < 2):
                    pe.wait_ge(f_y1, t)
                for c in range(2 * HC):
                    mm = nc.tensor.matmul(bank[1 + u][:, 0:C], hidT[:, u, c * P:(c + 1) * P],
                                          w2_all[:, ds(e * (2 * HC * C) + c * C, C)], start=(c == 0), stop=(c == 2 * HC - 1))
                mm.then_inc(f_y, 1)

            pe.wait_ge(s_w2, 16)
            pe.wait_ge(s_slots, 1)
            rows(0)
            rows(1)
            hidden(0, 0)
            rows(2)
            hidden(1, 1)
            second(0, 0)
            with pe.Fori(1, FT // 2) as i:
                rows(2 * i + 1)
                hidden(2 * i, 0)
                second(2 * i - 1, 1)
                rows(2 * i + 2)
                hidden(2 * i + 1, 1)
                second(2 * i, 0)
            hidden(FT - 1, 0)
            second(FT - 2, 1)
            second(FT - 1, 0)


def kernel(x, src, dst, L0_gnn_weight, L0_gnn_attn_l, L0_gnn_attn_r, L0_mix_Wqkv, L0_mix_Wproj, L0_mix_bproj,
           L0_mix_ln_g, L0_mix_ln_b, L0_mix_Wg1, L0_mix_bg1, L0_mix_Wg2, L0_mix_bg2, L0_ffn_Wr, L0_ffn_br,
           L0_ffn_ln_g, L0_ffn_ln_b, L0_ffn_W1, L0_ffn_b1, L0_ffn_W2, L0_ffn_b2):
    import numpy as np
    import concourse.bacc as bacc
    from concourse.bass_utils import run_bass_kernel_spmd as run

    def chunks(w):
        w = np.asarray(w)
        return w.reshape(-1, P, w.shape[-1]).transpose(1, 0, 2)

    def rows(v):
        v = np.asarray(v).reshape(1, -1)
        return np.broadcast_to(v, (P, v.shape[1]))

    def columns(v):
        v = np.asarray(v)
        v = v.reshape(-1, NK, P).transpose(2, 1, 0)
        return v.reshape(P, -1)

    def tokens(a):
        padded = np.zeros(NP, np.asarray(a).dtype)
        padded[:N] = np.asarray(a)[:N]
        return padded.reshape(NT, P).T

    wqkv = np.asarray(L0_mix_Wqkv)
    xp = np.zeros((NP, C), np.float32)
    xp[:N] = np.asarray(x)
    attn = np.stack([np.asarray(L0_gnn_attn_l).reshape(-1), np.asarray(L0_gnn_attn_r).reshape(-1)])
    w1 = np.asarray(L0_ffn_W1).reshape(NE, NK, P, HID).transpose(2, 0, 1, 3).reshape(P, -1)
    w2 = np.asarray(L0_ffn_W2).reshape(NE, HID // P, P, C).transpose(2, 0, 1, 3).reshape(P, -1)
    vecs = np.stack([columns(v) for v in (L0_mix_ln_g, L0_mix_ln_b, L0_mix_bg2)], axis=1)
    arrays = {
        "x": xp, "edges": np.stack([tokens(dst), tokens(src)], axis=2).reshape(P, -1),
        "wk": chunks(wqkv[:, C:2 * C]), "wqT": chunks(wqkv[:, 0:C].T), "wv": chunks(wqkv[:, 2 * C:3 * C]),
        "wgnn": chunks(L0_gnn_weight), "attn": np.broadcast_to(attn[None], (P, 2, C)),
        "wproj": chunks(L0_mix_Wproj), "bproj": rows(L0_mix_bproj), "vecs": vecs,
        "wg1": chunks(L0_mix_Wg1), "bg1": rows(L0_mix_bg1), "wg2": np.asarray(L0_mix_Wg2),
        "wr": chunks(L0_ffn_Wr), "br": rows(L0_ffn_br), "flng": columns(L0_ffn_ln_g), "flnb": columns(L0_ffn_ln_b),
        "w1": w1, "b1": np.asarray(L0_ffn_b1).reshape(-1, P).T, "w2": w2, "b2": rows(L0_ffn_b2),
    }
    arrays = {k: np.ascontiguousarray(a) for k, a in arrays.items()}
    nc = bacc.Bacc("TRN2", target_bir_lowering=False, num_devices=1)
    args = {k: nc.dram_tensor(k + "_in", a.shape, mybir.dt.from_np(a.dtype), kind="ExternalInput").ap()
            for k, a in arrays.items()}
    fp32 = mybir.dt.float32
    args["out"] = nc.dram_tensor("rows_out", (NP + P, C), fp32, kind="ExternalOutput").ap()
    for name, shape in (("xt_table", (NP, ROW)), ("al_table", (NP, HG)), ("x4_table", (NP, C)),
                        ("xb_table", (NP, C))):
        args[name] = nc.dram_tensor(name, shape, fp32, kind="Internal").ap()
    gps_layer(nc, **args)
    r = run(nc, [{k + "_in": a for k, a in arrays.items()}], core_ids=[0])
    return np.asarray(r.results[0]["rows_out"])[:N]
```
